# Optimizing a Trainium2 kernel written in Bass

```python
import numpy as np
import jax
import jax.numpy as jnp

def _softmax(x, axis=-1):
    return jax.nn.softmax(x, axis=axis)

def _gelu(x):
    return jax.nn.gelu(x, approximate=True)

def _silu(x):
    return jax.nn.silu(x)

def _sigmoid(x):
    return jax.nn.sigmoid(x)

def _layernorm(x, axis=-1, eps=1e-05):
    m = jnp.mean(x, axis=axis, keepdims=True)
    v = jnp.var(x, axis=axis, keepdims=True)
    return (x - m) / jnp.sqrt(v + eps)

def _scatter_add(tgt, idx, src, axis=0):
    return tgt.at[idx].add(src)

def _segment_sum(src, seg, n):
    return jax.ops.segment_sum(src, seg, n)
kernel_name = 'mk_vit_tower_d1_tok_img1024_r4_a23098'

def setup_inputs(seed: int=0):
    np.random.seed(seed)
    _w = jnp.asarray

    def _rec_inputs():
        import jax
        import jax.numpy as jnp
        _rk = jax.random.key(seed)
        x = -0.00016672 + 0.999947 * jax.random.normal(jax.random.fold_in(_rk, 1), (64, 3, 64, 64), jnp.float32)
        return x
    x = _rec_inputs()

    def _L0_tok_setup():
        import jax, jax.numpy as jnp
        import numpy as np
        PATCH = 16
        D_MODEL = 256

        def patchify(imgs, p):
            n, c, H, W = imgs.shape
            h, w = (H // p, W // p)
            x = imgs.reshape(n, c, h, p, w, p)
            x = jnp.einsum('nchpwq->nhwpqc', x)
            return x.reshape(n, h * w, p * p * c)
        key = jax.random.key(seed)
        k1, k2, k3 = jax.random.split(key, 3)
        val = jax.random.normal(k1, (64, 3, 96, 96), dtype=jnp.float32)
        in_dim = PATCH * PATCH * 3
        bound = 1.0 / np.sqrt(in_dim)
        W = jax.random.uniform(k2, (D_MODEL, in_dim), dtype=jnp.float32, minval=-bound, maxval=bound)
        b = jax.random.uniform(k3, (D_MODEL,), dtype=jnp.float32, minval=-bound, maxval=bound)
        return {'val': val, 'W': W, 'b': b}
    _L0_tok_all = _L0_tok_setup()
    _L0_tok_in = {k: v for k, v in _L0_tok_all.items() if k in ('W', 'b')}
    del _L0_tok_all

    def _L0_attn_setup():
        import jax, jax.numpy as jnp
        import numpy as np
        import math
        DIM = 256
        NUM_HEADS = 16
        HEAD_DIM = DIM // NUM_HEADS
        LAYER_IDX = 12
        LAMBDA_INIT = 0.8 - 0.6 * math.exp(-0.3 * (LAYER_IDX - 1))
        LN_EPS = 1e-05
        key = jax.random.key(seed)
        ks = jax.random.split(key, 11)
        B, S = (2, 512)
        x = jax.random.normal(ks[0], (B, S, DIM), dtype=jnp.float32)
        s = 1.0 / math.sqrt(DIM)
        Wq = jax.random.normal(ks[1], (DIM, 2 * DIM), dtype=jnp.float32) * s
        Wk = jax.random.normal(ks[2], (DIM, 2 * DIM), dtype=jnp.float32) * s
        Wv = jax.random.normal(ks[3], (DIM, DIM), dtype=jnp.float32) * s
        Wo = jax.random.normal(ks[4], (DIM, DIM), dtype=jnp.float32) * s
        lambda_q1 = jax.random.normal(ks[5], (HEAD_DIM,), dtype=jnp.float32) * 0.1
        lambda_k1 = jax.random.normal(ks[6], (HEAD_DIM,), dtype=jnp.float32) * 0.1
        lambda_q2 = jax.random.normal(ks[7], (HEAD_DIM,), dtype=jnp.float32) * 0.1
        lambda_k2 = jax.random.normal(ks[8], (HEAD_DIM,), dtype=jnp.float32) * 0.1
        gamma = jnp.ones((DIM,), dtype=jnp.float32)
        beta = jnp.zeros((DIM,), dtype=jnp.float32)
        return {'x': x, 'Wq': Wq, 'Wk': Wk, 'Wv': Wv, 'Wo': Wo, 'lambda_q1': lambda_q1, 'lambda_k1': lambda_k1, 'lambda_q2': lambda_q2, 'lambda_k2': lambda_k2, 'gamma': gamma, 'beta': beta}
    _L0_attn_all = _L0_attn_setup()
    _L0_attn_in = {k: v for k, v in _L0_attn_all.items() if k in ('Wq', 'Wk', 'Wv', 'Wo', 'lambda_q1', 'lambda_k1', 'lambda_q2', 'lambda_k2', 'gamma', 'beta')}
    del _L0_attn_all

    def _L0_ffn_setup():
        import math
        import jax, jax.numpy as jnp
        import numpy as np
        B, S, D, H, E, K = (4, 512, 256, 1024, 8, 2)
        CAPACITY_RATIO = 1.05
        key = jax.random.key(seed)
        k0, k1, k2, k3 = jax.random.split(key, 4)
        x = jax.random.normal(k0, (B, S, D), jnp.float32)
        Wg = jax.random.normal(k1, (D, E), jnp.float32) * 0.02
        W1 = jax.random.normal(k2, (E, D, H), jnp.float32) * 0.02
        b1 = jnp.zeros((E, H), jnp.float32)
        W2 = jax.random.normal(k3, (E, H, D), jnp.float32) * 0.02
        b2 = jnp.zeros((E, D), jnp.float32)
        return {'x': x, 'Wg': Wg, 'W1': W1, 'b1': b1, 'W2': W2, 'b2': b2}
    _L0_ffn_all = _L0_ffn_setup()
    _L0_ffn_in = {k: v for k, v in _L0_ffn_all.items() if k in ('Wg', 'W1', 'b1', 'W2', 'b2')}
    del _L0_ffn_all
    return {'x': x, 'L0_tok_W': _L0_tok_in['W'], 'L0_tok_b': _L0_tok_in['b'], 'L0_attn_Wq': _L0_attn_in['Wq'], 'L0_attn_Wk': _L0_attn_in['Wk'], 'L0_attn_Wv': _L0_attn_in['Wv'], 'L0_attn_Wo': _L0_attn_in['Wo'], 'L0_attn_lambda_q1': _L0_attn_in['lambda_q1'], 'L0_attn_lambda_k1': _L0_attn_in['lambda_k1'], 'L0_attn_lambda_q2': _L0_attn_in['lambda_q2'], 'L0_attn_lambda_k2': _L0_attn_in['lambda_k2'], 'L0_attn_gamma': _L0_attn_in['gamma'], 'L0_attn_beta': _L0_attn_in['beta'], 'L0_ffn_Wg': _L0_ffn_in['Wg'], 'L0_ffn_W1': _L0_ffn_in['W1'], 'L0_ffn_b1': _L0_ffn_in['b1'], 'L0_ffn_W2': _L0_ffn_in['W2'], 'L0_ffn_b2': _L0_ffn_in['b2']}

def reference(x, L0_tok_W, L0_tok_b, L0_attn_Wq, L0_attn_Wk, L0_attn_Wv, L0_attn_Wo, L0_attn_lambda_q1, L0_attn_lambda_k1, L0_attn_lambda_q2, L0_attn_lambda_k2, L0_attn_gamma, L0_attn_beta, L0_ffn_Wg, L0_ffn_W1, L0_ffn_b1, L0_ffn_W2, L0_ffn_b2):
    import jax
    import jax.numpy as jnp

    def _L0_tok_ref(val, W, b):
        import jax, jax.numpy as jnp
        import numpy as np
        PATCH = 16
        D_MODEL = 256

        def patchify(imgs, p):
            n, c, H, W = imgs.shape
            h, w = (H // p, W // p)
            x = imgs.reshape(n, c, h, p, w, p)
            x = jnp.einsum('nchpwq->nhwpqc', x)
            return x.reshape(n, h * w, p * p * c)
        patches = patchify(val, PATCH)
        return jnp.einsum('nld,md->nlm', patches, W) + b

    def _L0_attn_ref(x, Wq, Wk, Wv, Wo, lambda_q1, lambda_k1, lambda_q2, lambda_k2, gamma, beta):
        import jax, jax.numpy as jnp
        import numpy as np
        import math
        DIM = 256
        NUM_HEADS = 16
        HEAD_DIM = DIM // NUM_HEADS
        LAYER_IDX = 12
        LAMBDA_INIT = 0.8 - 0.6 * math.exp(-0.3 * (LAYER_IDX - 1))
        LN_EPS = 1e-05
        B, S, _ = x.shape
        scaling = HEAD_DIM ** (-0.5)
        Q = (x @ Wq).reshape(B, S, NUM_HEADS, 2 * HEAD_DIM).transpose(0, 2, 1, 3)
        K = (x @ Wk).reshape(B, S, NUM_HEADS, 2 * HEAD_DIM).transpose(0, 2, 1, 3)
        V = (x @ Wv).reshape(B, S, NUM_HEADS, HEAD_DIM).transpose(0, 2, 1, 3)
        lamb = jnp.exp(jnp.sum(lambda_q1 * lambda_k1)) - jnp.exp(jnp.sum(lambda_q2 * lambda_k2)) + LAMBDA_INIT
        Q1, Q2 = jnp.split(Q, 2, axis=-1)
        K1, K2 = jnp.split(K, 2, axis=-1)
        A1 = jnp.einsum('bhqd,bhkd->bhqk', Q1, K1) * scaling
        A2 = jnp.einsum('bhqd,bhkd->bhqk', Q2, K2) * scaling
        attn = jax.nn.softmax(A1, axis=-1) - lamb * jax.nn.softmax(A2, axis=-1)
        out = jnp.einsum('bhqk,bhkd->bhqd', attn, V)
        out = out.transpose(0, 2, 1, 3).reshape(B, S, DIM)
        out = out @ Wo
        mu = jnp.mean(out, axis=-1, keepdims=True)
        var = jnp.var(out, axis=-1, keepdims=True)
        out = (out - mu) * jax.lax.rsqrt(var + LN_EPS) * gamma + beta
        return out

    def _L0_ffn_ref(x, Wg, W1, b1, W2, b2):
        import math
        import jax, jax.numpy as jnp
        import numpy as np
        B, S, D, H, E, K = (4, 512, 256, 1024, 8, 2)
        CAPACITY_RATIO = 1.05
        b, s, d = x.shape
        e = Wg.shape[1]
        n = b * s
        cap = int(math.ceil(n * K / e * CAPACITY_RATIO))
        xf = x.reshape(n, d)
        probs = jax.nn.softmax(xf @ Wg, axis=-1)
        topv, topi = jax.lax.top_k(probs, K)
        gates = topv / jnp.sum(topv, axis=-1, keepdims=True)
        eidx = topi.reshape(-1)
        oh = jax.nn.one_hot(eidx, e, dtype=jnp.int32)
        pos = jnp.sum(jnp.cumsum(oh, axis=0) * oh, axis=-1) - 1
        keep = pos < cap
        dest = jnp.where(keep, eidx * cap + pos, e * cap)
        xr = jnp.repeat(xf, K, axis=0)
        buf = jnp.zeros((e * cap + 1, d), x.dtype).at[dest].set(xr)
        expert_in = buf[:e * cap].reshape(e, cap, d)
        h = jax.nn.gelu(jnp.einsum('ecd,edh->ech', expert_in, W1) + b1[:, None, :])
        y = jnp.einsum('ech,ehd->ecd', h, W2) + b2[:, None, :]
        yf = jnp.concatenate([y.reshape(e * cap, d), jnp.zeros((1, d), y.dtype)], axis=0)
        gathered = yf[dest]
        w = (gates.reshape(-1) * keep.astype(gates.dtype))[:, None]
        out = (gathered * w).reshape(n, K, d).sum(axis=1).reshape(b, s, d)
        return out
    h = _L0_tok_ref(x, L0_tok_W, L0_tok_b)
    h = h + _L0_attn_ref(_layernorm(h, axis=-1), L0_attn_Wq, L0_attn_Wk, L0_attn_Wv, L0_attn_Wo, L0_attn_lambda_q1, L0_attn_lambda_k1, L0_attn_lambda_q2, L0_attn_lambda_k2, L0_attn_gamma, L0_attn_beta)
    h = h + _L0_ffn_ref(_layernorm(h, axis=-1), L0_ffn_Wg, L0_ffn_W1, L0_ffn_b1, L0_ffn_W2, L0_ffn_b2)
    return h

_drawn_inputs = setup_inputs


def setup_inputs(seed=0):
    import zlib

    import numpy as np

    out = dict(_drawn_inputs(seed))
    spreads = {'L0_attn_gamma': (1.0, 0.2),
     'L0_attn_beta': (0.0, 0.1),
     'L0_ffn_b1': (0.0, 0.364),
     'L0_ffn_b2': (0.0, 0.1)}
    factors = {'L0_attn_lambda_q1': 3.967, 'L0_attn_lambda_q2': 3.129}
    for name, (base, spread) in spreads.items():
        noise = np.random.default_rng([zlib.crc32(name.encode()), seed]).standard_normal(out[name].shape)
        drawn = base * np.exp(spread * noise) if base else spread * noise
        out[name] = jnp.asarray(drawn.astype(out[name].dtype))
    for name, factor in factors.items():
        out[name] = (out[name] * factor).astype(out[name].dtype)
    return out
```

```python
import numpy as np
import concourse.bass as bass
from concourse import mybir
from contextlib import ExitStack
import math

F32 = mybir.dt.float32
U32 = mybir.dt.uint32
ALU = mybir.AluOpType
ACT = mybir.ActivationFunctionType
AX = mybir.AxisListType

P = 128
IMGS, CH, SIDE, PATCH = 64, 3, 64, 16
S = (SIDE // PATCH) ** 2
N = IMGS * S
G = N // P
GI = P // S
D = 256
DC = D // P
IN = PATCH * PATCH * CH
IC = IN // P
HEADS, HD = 16, 16
QC = 2 * D // P
HB = P // HD
NHB = 2 * HEADS
SCALE = HD ** -0.5
LAMBDA_INIT = 0.8 - 0.6 * math.exp(-0.3 * 11)
EPS = 1e-5
E, K, HID = 8, 2, 1024
HC = HID // P
CAP = int(math.ceil(N * K / E * 1.05))
SLOTS = E * CAP
XT = -(-SLOTS // P)
YT = [(t, min(P, CAP - t)) for t in range(0, CAP, P)]
NY = len(YT)


def vit_tower(nc, xh, wt, tok_b, wq, wk, wv, wo, lam, gamma, beta, wg, w1, b1, w2, b2, out):
    ctx = ExitStack()
    with ctx:
        def sb(name, shape, dt=F32):
            return ctx.enter_context(nc.sbuf_tensor(name, shape, dt))

        def sem(name):
            return ctx.enter_context(nc.semaphore(name))

        xbuf = nc.dram_tensor("xbuf", (SLOTS + K * N, D), F32, kind="Internal").ap()
        ybuf = nc.dram_tensor("ybuf", (SLOTS + 1, D), F32, kind="Internal").ap()

        front = sb("front", [P, G * IC * P])
        x_sb = front[:, :].rearrange("p (g c t) -> p g c t", g=G, c=IC)
        xg = front[:, 0:XT * D].rearrange("p (t d) -> p t d", t=XT)
        wt_sb = sb("wt_sb", [P, IC, D])
        wq_sb = sb("wq_sb", [P, DC, 2 * D])
        wk_sb = sb("wk_sb", [P, DC, 2 * D])
        wv_sb = sb("wv_sb", [P, DC, D])
        wo_sb = sb("wo_sb", [P, DC, D])
        wg_sb = sb("wg_sb", [P, DC, E])
        b1_sb = sb("b1_sb", [P, E, HC])
        b2_sb = sb("b2_sb", [P, E, DC])
        rows = sb("rows", [P, 3, D])
        lam_sb = sb("lam_sb", [P, 2, 2, HD])
        lam_pr = sb("lam_pr", [P, 2, HD])
        lam_s = sb("lam_s", [P, 2])
        lam_e = sb("lam_e", [P, 2])
        neglam = sb("neglam", [P, 2])
        ident = sb("ident", [P, P])
        same = sb("same", [P, GI, S])
        upper = sb("upper", [P, P])
        ones = sb("ones", [P, P])
        half = sb("half", [P, 1])
        iota8 = sb("iota8", [P, E])
        trash = sb("trash", [P, G, K])
        zero = sb("zero", [P, D])
        h_sb = sb("h_sb", [P, G, D])
        xn = sb("xn", [P, 2, D])
        xnT = sb("xnT", [P, DC, N])
        qT = sb("qT", [P, 2, QC, P])
        kT = sb("kT", [P, QC * GI, S])
        v_sb = sb("v_sb", [P, 2, D])
        big = sb("big", [P, QC * GI * P + HEADS * P])
        kblk = big[:, 0:QC * GI * P].rearrange("p (a j s) -> p a j s", j=HB, s=S)
        pf = big[:, QC * GI * P:].rearrange("p (h t) -> p h t", h=HEADS)
        hT = big[:, 0:2 * HC * CAP].rearrange("p (r j s) -> p r j s", r=2, j=HC)
        sT = sb("sT", [P, QC, P])
        sd = sb("sd", [P, NHB, S])
        ex = sb("ex", [P, NHB, S])
        prob = sb("prob", [P, HEADS, S])
        pw = sb("pw", [P, HEADS, GI, S])
        o_sb = sb("o_sb", [P, D])
        oT = sb("oT", [P, DC, P])
        t1 = sb("t1", [P, D])
        t2 = sb("t2", [P, D])
        x2T = sb("x2T", [P, DC, P])
        xrow = sb("xrow", [P, 2, D])
        stat = sb("stat", [P, 2, 6])
        mv = sb("mv", [P, 2, 2])
        var = sb("var", [P, 2])
        rstd = sb("rstd", [P, 2])
        stat1 = sb("stat1", [P, 2, 6])
        mv1 = sb("mv1", [P, 2, 2])
        var1 = sb("var1", [P, 2])
        rstd1 = sb("rstd1", [P, 2])
        mx = sb("mx", [P, NHB])
        sm = sb("sm", [P, NHB])
        rc = sb("rc", [P, NHB])
        lmax = sb("lmax", [P, 8])
        ld = sb("ld", [P, E])
        le = sb("le", [P, E])
        top = sb("top", [P, 8])
        topi = sb("topi", [P, 8], U32)
        topf = sb("topf", [P, K])
        oh = sb("oh", [P, K, E])
        sel = sb("sel", [P, E])
        prev = sb("prev", [P, E])
        gs = sb("gs", [P, 2])
        gate = sb("gate", [P, K])
        junk = sb("junk", [P, K, E])
        pos = sb("pos", [P, K])
        keep = sb("keep", [P, K])
        dest = sb("dest", [P, K])
        dsc = sb("dsc", [P, 2, K])
        send = sb("send", [P, G, K], U32)
        fetch = sb("fetch", [P, G, K], U32)
        w_sb = sb("w_sb", [P, G, K])
        w1_sb = sb("w1_sb", [P, 2, DC, HID])
        w2_sb = sb("w2_sb", [P, 2, HC, D])
        xT = sb("xT", [P, DC, SLOTS])
        yT = sb("yT", [P, 2, DC, CAP])
        yr = sb("yr", [P, 2, NY, D])
        got = sb("got", [P, 2, K, D])
        fin = sb("fin", [P, 2, D])

        bank = [ctx.enter_context(nc.psum_tensor(f"bank{i}", [P, 512], F32)) for i in range(8)]

        x_in = [sem(f"x_in{g}") for g in range(G)]
        wt_in, rows_in, lam_in, wqk_in, wvo_in, small_in = (sem(n) for n in (
            "wt_in", "rows_in", "lam_in", "wqk_in", "wvo_in", "small_in"))
        zeroed = sem("zeroed")
        w1_in = [sem(f"w1_in{i}") for i in range(2)]
        w2_in = [sem(f"w2_in{i}") for i in range(2)]
        xg_in = sem("xg_in")
        made, lam_dve, lam_exp = sem("made"), sem("lam_dve"), sem("lam_exp")
        step = sem("step")
        emb_done, h_ready, ln1_var, ln1_rstd, xn_ready, xnt_done, xnt_ready = (sem(n) for n in (
            "emb_done", "h_ready", "ln1_var", "ln1_rstd", "xn_ready", "xnt_done", "xnt_ready"))
        q_done, k_done, v_done, q_ready, k_ready, v_ready, kblk_dve, kblk_pool = (sem(n) for n in (
            "q_done", "k_done", "v_done", "q_ready", "k_ready", "v_ready", "kblk_dve", "kblk_pool"))
        st_done, st_ready, s_done, sd_ready, ex_ready, p_ready, pt_done, pf_ready, pv_done = (sem(n) for n in (
            "st_done", "st_ready", "s_done", "sd_ready", "ex_ready", "p_ready", "pt_done", "pf_ready", "pv_done"))
        pw_dve, pw_pool = sem("pw_dve"), sem("pw_pool")
        o_ready, ot_done, ot_ready, wo_done, wo_read = (sem(n) for n in (
            "o_ready", "ot_done", "ot_ready", "wo_done", "wo_read"))
        lno_var, lno_rstd, ln2_var, ln2_rstd, x2_ready, x2t_done, x2t_ready, lg_done, ld_ready, le_ready = (
            sem(n) for n in ("lno_var", "lno_rstd", "ln2_var", "ln2_rstd", "x2_ready", "x2t_done",
                             "x2t_ready", "lg_done", "ld_ready", "le_ready"))
        sel_ready, prev_ready, cum_done, cum_read, send_ready = (sem(n) for n in (
            "sel_ready", "prev_ready", "cum_done", "cum_read", "send_ready"))
        sent = [sem(f"sent{i}") for i in range(2)]
        xt_done, xt_ready, l1_done, h_done, l2_done, yt_ready, yr_done, yr_ready = (sem(n) for n in (
            "xt_done", "xt_ready", "l1_done", "h_done", "l2_done", "yt_ready", "yr_done", "yr_ready"))
        stored = [sem(f"stored{i}") for i in range(2)]
        fetched = [sem(f"fetched{i}") for i in range(2)]
        fin_ready = sem("fin_ready")
        out_done = [sem(f"out_done{i}") for i in range(2)]

        block = ctx.enter_context(nc.Block())

        def expert_loop(eng, body):
            for r in range(2):
                body(r, r, r == 0)
            with eng.Fori(1, E // 2) as i:
                for r in range(2):
                    body(i * 2 + r, r, False)

        @block.sync
        def _(sp):
            sp.dma_start(x_sb[:, 0, :, :], xh[:, 0, :, :]).then_inc(x_in[0], 16)
            sp.dma_start(wt_sb[:, :, :], wt).then_inc(wt_in, 16)
            for n, r in enumerate((tok_b, gamma, beta)):
                sp.dma_start(rows[:, n, :], r.partition_broadcast(P)).then_inc(rows_in, 16)
            for g in range(1, G):
                sp.dma_start(x_sb[:, g, :, :], xh[:, g, :, :]).then_inc(x_in[g], 16)
            sp.dma_start(wq_sb[:, :, :], wq).then_inc(wqk_in, 16)
            sp.dma_start(wk_sb[:, :, :], wk).then_inc(wqk_in, 16)
            sp.dma_start(wv_sb[:, :, :], wv).then_inc(wvo_in, 16)
            sp.dma_start(wo_sb[:, :, :], wo).then_inc(wvo_in, 16)
            sp.dma_start(lam_sb[:, :, :, :], lam.partition_broadcast(P)).then_inc(lam_in, 16)
            for t, s in ((wg_sb, wg), (b1_sb, b1), (b2_sb, b2)):
                sp.dma_start(t[:, :, :], s).then_inc(small_in, 16)
            sp.wait_ge(made, 1)
            for t in range(XT):
                n = min(P, SLOTS - t * P)
                sp.dma_start(xbuf[t * P:t * P + n, :], zero[0:n, :]).then_inc(zeroed, 16)
            sp.dma_start(ybuf[SLOTS:SLOTS + 1, :], zero[0:1, :]).then_inc(zeroed, 16)
            for e in range(2):
                sp.dma_start(w1_sb[:, e, :, :], w1[e, :, :, :]).then_inc(w1_in[e], 16)
                sp.dma_start(w2_sb[:, e, :, :], w2[e, :, :, :]).then_inc(w2_in[e], 16)
            for r in range(2):
                sp.wait_ge(sent[r], 16 * K * (G // 2))
            for t in range(XT):
                n = min(P, SLOTS - t * P)
                sp.dma_start(xg[0:n, t, :], xbuf[t * P:t * P + n, :]).then_inc(xg_in, 16)

            def stage(e, r, first):
                sp.wait_ge(l2_done, (e + 1) * DC)
                sp.dma_start(w1_sb[:, r, :, :], w1[e + 2, :, :, :]).then_inc(w1_in[r], 16)
                sp.dma_start(w2_sb[:, r, :, :], w2[e + 2, :, :, :]).then_inc(w2_in[r], 16)
                store(e, r)

            def store(e, r):
                sp.wait_ge(yr_ready, (e + 1) * NY)
                for t, (s0, n) in enumerate(YT):
                    sp.dma_start(ybuf[bass.ds(e * CAP + s0, n), :], yr[0:n, r, t, :]).then_inc(stored[r], 16)

            for r in range(2):
                stage(r, r, False)
            with sp.Fori(1, E // 2 - 1) as i:
                for r in range(2):
                    stage(i * 2 + r, r, False)
            for e in (E - 2, E - 1):
                store(e, e % 2)
            for g in range(G):
                sp.wait_ge(fin_ready, g + 1)
                sp.dma_start(out[g * P:(g + 1) * P, :], fin[:, g % 2, :]).then_inc(out_done[g % 2], 16)
            for r in range(2):
                sp.wait_ge(out_done[r], 16 * (G // 2))

        @block.gpsimd
        def _(pool):
            pool.memset(zero[:, :], 0.0).then_inc(made, 1)
            pool.memset(ident[:, :], 0.0).then_inc(made, 1)
            pool.memset(same[:, :, :], 1.0).then_inc(made, 1)
            pool.memset(upper[:, :], 1.0).then_inc(made, 1)
            pool.memset(ones[:, :], 1.0).then_inc(made, 1)
            pool.memset(half[:, :], -0.5).then_inc(made, 1)
            pool.memset(prev[:, :], 0.0).then_inc(made, 1)
            pool.iota(iota8[:, :], pattern=[[1, E]], base=0, channel_multiplier=0,
                      allow_small_or_imprecise_dtypes=True).then_inc(made, 1)
            pool.iota(trash[:, :, :], pattern=[[K * P, G], [P, K]], base=SLOTS, channel_multiplier=1,
                      allow_small_or_imprecise_dtypes=True).then_inc(made, 1)
            pool.wait_ge(made, 9)
            pool.affine_select(out=ident[:, :], in_=ident[:, :], compare_op=ALU.not_equal, fill=1.0, base=0,
                               pattern=[[-1, P]], channel_multiplier=1).then_inc(made, 1)
            pool.affine_select(out=same[:, :, :], in_=same[:, :, :], compare_op=ALU.is_ge, fill=0.0, base=0,
                               pattern=[[-S, GI], [0, S]], channel_multiplier=1).then_inc(made, 1)
            pool.wait_ge(made, 11)
            pool.affine_select(out=same[:, :, :], in_=same[:, :, :], compare_op=ALU.is_ge, fill=0.0, base=S - 1,
                               pattern=[[S, GI], [0, S]], channel_multiplier=-1).then_inc(made, 1)
            pool.affine_select(out=upper[:, :], in_=upper[:, :], compare_op=ALU.is_gt, fill=0.0, base=0,
                               pattern=[[1, P]], channel_multiplier=-1).then_inc(made, 1)
            pool.wait_ge(made, 13)

            def power(var_sem, rstd_sem, src, dst, g):
                pool.wait_ge(var_sem, g + 1)
                pool.tensor_tensor(dst, src, half[:, :], ALU.pow).then_inc(rstd_sem, 1)

            for g in range(G):
                power(ln1_var, ln1_rstd, var1[:, g % 2:g % 2 + 1], rstd1[:, g % 2:g % 2 + 1], g)

            def tick(t):
                b, g = t - 1, t - 2
                if g >= 0:
                    power(lno_var, lno_rstd, var[:, 0:1], rstd[:, 0:1], g)
                if t < G:
                    pool.wait_ge(k_ready, t + 1)
                    for j in range(KDVE, HB):
                        ins = pool.tensor_scalar(kblk[:, :, j, :], kT[:, :, :], same[:, j, 0:1], None, ALU.mult)
                    ins.then_inc(kblk_pool, 1)
                if g >= 0:
                    power(ln2_var, ln2_rstd, var[:, 1:2], rstd[:, 1:2], g)
                if 0 <= b < G:
                    pool.wait_ge(p_ready, b + 1)
                    for a in range(WDVE, GI):
                        ins = pool.tensor_scalar(pw[:, :, a, :], prob[:, :, :], same[:, a, 0:1], None, ALU.mult)
                    ins.then_inc(pw_pool, 1)
                if g >= 0:
                    if g == 0:
                        pool.wait_ge(zeroed, 16 * (XT + 1))
                    pool.wait_ge(send_ready, g + 1)
                    for k in range(K):
                        pool.indirect_dma_start(
                            out=xbuf[:, :], out_offset=bass.IndirectOffsetOnAxis(ap=send[:, g, k:k + 1], axis=0),
                            in_=xrow[:, g % 2, :], in_offset=None).then_inc(sent[g % 2], 16)

            for t in range(G + 2):
                tick(t)
            for r in range(2):
                pool.wait_ge(stored[r], 16 * NY * (E // 2))
            for g in range(G):
                if g >= 2:
                    pool.wait_ge(fin_ready, g - 1)
                for k in range(K):
                    pool.indirect_dma_start(
                        out=got[:, g % 2, k, :], out_offset=None, in_=ybuf[:, :],
                        in_offset=bass.IndirectOffsetOnAxis(ap=fetch[:, g, k:k + 1], axis=0)).then_inc(fetched[g % 2], 16)

        @block.scalar
        def _(act):
            act.wait_ge(lam_dve, 1)
            act.activation(lam_e[:, :], lam_s[:, :], ACT.Exp).then_inc(lam_exp, 1)
            for g in range(G):
                act.wait_ge(xnt_done, g + 1)
                act.activation(xnT[:, :, g * P:(g + 1) * P],
                               bank[2 + g % 2][:, 0:D].rearrange("p (c t) -> p c t", c=DC), ACT.Copy).then_inc(xnt_ready, 1)

            def tick(t):
                a, b, c = t, t - 1, t - 2
                if 0 <= b < G:
                    act.wait_ge(st_done, b + 1)
                    act.activation(sT[:, :, :], bank[3][:, :], ACT.Copy).then_inc(st_ready, 1)
                if a < G:
                    act.wait_ge(q_done, a + 1)
                    act.activation(qT[:, a % 2, :, :], bank[0][:, :], ACT.Copy).then_inc(q_ready, 1)
                    act.wait_ge(k_done, a + 1)
                    if a >= 1:
                        act.wait_ge(kblk_dve, a)
                        act.wait_ge(kblk_pool, a)
                    act.activation(kT[:, :, :], bank[1][:, :], ACT.Copy).then_inc(k_ready, 1)
                if 0 <= b < G:
                    act.wait_ge(sd_ready, b + 1)
                    act.activation(ex[:, :, :], sd[:, :, :], ACT.Exp, scale=SCALE).then_inc(ex_ready, 1)
                if a < G:
                    act.wait_ge(v_done, a + 1)
                    if a >= 2:
                        act.wait_ge(pv_done, a - 1)
                    act.activation(v_sb[:, a % 2, :], bank[2][:, 0:D], ACT.Copy).then_inc(v_ready, 1)
                if c >= 0:
                    act.wait_ge(x2t_done, c + 1)
                    act.activation(x2T[:, :, :], bank[7][:, 0:D], ACT.Copy).then_inc(x2t_ready, 1)
                    act.wait_ge(ld_ready, c + 1)
                    act.activation(le[:, :], ld[:, :], ACT.Exp).then_inc(le_ready, 1)
                if 0 <= b < G:
                    for n in range(4):
                        act.wait_ge(pt_done, 4 * b + n + 1)
                        act.activation(pf[:, 4 * n:4 * n + 4, :], bank[4 + n % 2][:, :], ACT.Copy).then_inc(pf_ready, 1)
                    act.wait_ge(pv_done, b + 1)
                    act.activation(o_sb[:, :], bank[6][:, 0:D], ACT.Copy).then_inc(o_ready, 1)
                    act.wait_ge(ot_done, b + 1)
                    act.activation(oT[:, :, :], bank[6][:, D:2 * D], ACT.Copy).then_inc(ot_ready, 1)

            for t in range(G + 2):
                tick(t)
            for t in range(XT):
                n = min(P, SLOTS - t * P)
                act.wait_ge(xt_done, t + 1)
                act.activation(xT[:, :, t * P:t * P + n],
                               bank[t % 4][:, 0:DC * n].rearrange("p (c s) -> p c s", c=DC), ACT.Copy).then_inc(xt_ready, 1)

            def expert(e, r, first):
                for j in range(HC):
                    act.wait_ge(l1_done, e * HC + j + 1)
                    act.activation(hT[:, r, j, :], bank[j % 4][:, 0:CAP], ACT.Gelu_apprx_tanh,
                                   bias=b1_sb[:, bass.ds(e, 1), j]).then_inc(h_done, 1)

            act.wait_ge(small_in, 48)
            act.wait_ge(xt_ready, XT)
            expert_loop(act, expert)

        @block.vector
        def _(dve):
            steps = [0]

            def then(ins):
                steps[0] += 1
                ins.then_inc(step, 1)
                dve.wait_ge(step, steps[0])

            dve.wait_ge(lam_in, 16)
            then(dve.tensor_tensor(lam_pr[:, :, :], lam_sb[:, :, 0, :], lam_sb[:, :, 1, :], ALU.mult))
            dve.reduce_sum(lam_s[:, :], lam_pr[:, :, :], AX.X).then_inc(lam_dve, 1)
            dve.wait_ge(lam_exp, 1)
            then(dve.tensor_tensor(neglam[:, 0:1], lam_e[:, 1:2], lam_e[:, 0:1], ALU.subtract))
            then(dve.tensor_scalar(neglam[:, 1:2], neglam[:, 0:1], -LAMBDA_INIT, None, ALU.add))
            dve.wait_ge(rows_in, 48)

            def embed_open(g):
                r = g % 2
                dve.wait_ge(emb_done, g + 1)
                dve.tensor_tensor(h_sb[:, g, :], bank[r][:, 0:D], rows[:, 0, :], ALU.add).then_inc(h_ready, 1)
                dve.wait_ge(h_ready, g + 1)
                then(dve.bn_stats(stat1[:, r, :], h_sb[:, g, :]))
                then(dve.bn_aggr(mv1[:, r, :], stat1[:, r, :]))
                dve.tensor_scalar(var1[:, r:r + 1], mv1[:, r, 1:2], EPS, None, ALU.add).then_inc(ln1_var, 1)

            def embed_close(g):
                r = g % 2
                dve.wait_ge(ln1_rstd, g + 1)
                if g >= 2:
                    dve.wait_ge(xnt_done, g - 1)
                dve.tensor_scalar(xn[:, r, :], h_sb[:, g, :], mv1[:, r, 0:1], rstd1[:, r:r + 1],
                                  ALU.subtract, ALU.mult).then_inc(xn_ready, 1)
                then(dve.tensor_tensor(h_sb[:, g, :], h_sb[:, g, :], rows[:, 2, :], ALU.add))

            for g in range(G + 1):
                if g < G:
                    embed_open(g)
                if g >= 1:
                    embed_close(g - 1)
            dve.wait_ge(made, 13)

            def softmax_open(g):
                s3 = bank[3][:, :].rearrange("p (a s) -> p a s", s=S)
                dve.wait_ge(s_done, g + 1)
                then(dve.reduce_max(mx[:, :], s3, AX.X))
                dve.tensor_tensor(sd[:, :, :], s3, mx[:, :].unsqueeze(2).broadcast_to([P, NHB, S]),
                                  ALU.subtract).then_inc(sd_ready, 1)

            def spread(g):
                dve.wait_ge(k_ready, g + 1)
                for j in range(KDVE):
                    ins = dve.tensor_scalar(kblk[:, :, j, :], kT[:, :, :], same[:, j, 0:1], None, ALU.mult)
                ins.then_inc(kblk_dve, 1)

            def softmax_close(g):
                dve.wait_ge(ex_ready, g + 1)
                then(dve.reduce_sum(sm[:, :], ex[:, :, :], AX.X))
                then(dve.reciprocal(rc[:, :], sm[:, :]))
                second = rc[:, :].rearrange("p (h b) -> p h b", b=2)[:, :, 1]
                then(dve.tensor_scalar(second, second, neglam[:, 1:2], None, ALU.mult))
                then(dve.tensor_tensor(ex[:, :, :], ex[:, :, :], rc[:, :].unsqueeze(2).broadcast_to([P, NHB, S]), ALU.mult))
                if g >= 1:
                    dve.wait_ge(pt_done, 4 * g)
                pair = ex[:, :, :].rearrange("p (h b) s -> p h b s", b=2)
                dve.tensor_tensor(prob[:, :, :], pair[:, :, 0, :], pair[:, :, 1, :], ALU.add).then_inc(p_ready, 1)

            def widen(g):
                dve.wait_ge(p_ready, g + 1)
                for a in range(WDVE):
                    ins = dve.tensor_scalar(pw[:, :, a, :], prob[:, :, :], same[:, a, 0:1], None, ALU.mult)
                ins.then_inc(pw_dve, 1)

            def norms_open(g):
                dve.wait_ge(wo_done, g + 1)
                then(dve.bn_stats(stat[:, 0, :], bank[6][:, 0:D]))
                then(dve.bn_aggr(mv[:, 0, :], stat[:, 0, :]))
                dve.tensor_scalar(var[:, 0:1], mv[:, 0, 1:2], EPS, None, ALU.add).then_inc(lno_var, 1)

            def norms_middle(g):
                dve.wait_ge(lno_rstd, g + 1)
                dve.tensor_scalar(t1[:, :], bank[6][:, 0:D], mv[:, 0, 0:1], rstd[:, 0:1],
                                  ALU.subtract, ALU.mult).then_inc(wo_read, 1)
                dve.wait_ge(wo_read, g + 1)
                then(dve.tensor_tensor(t2[:, :], t1[:, :], rows[:, 1, :], ALU.mult))
                then(dve.tensor_tensor(h_sb[:, g, :], t2[:, :], h_sb[:, g, :], ALU.add))
                then(dve.bn_stats(stat[:, 1, :], h_sb[:, g, :]))
                then(dve.bn_aggr(mv[:, 1, :], stat[:, 1, :]))
                dve.tensor_scalar(var[:, 1:2], mv[:, 1, 1:2], EPS, None, ALU.add).then_inc(ln2_var, 1)

            def norms_close(g):
                dve.wait_ge(ln2_rstd, g + 1)
                if g >= 2:
                    dve.wait_ge(sent[g % 2], 16 * K * (g // 2))
                dve.tensor_scalar(xrow[:, g % 2, :], h_sb[:, g, :], mv[:, 1, 0:1], rstd[:, 1:2],
                                  ALU.subtract, ALU.mult).then_inc(x2_ready, 1)

            def route_open(g):
                dve.wait_ge(lg_done, g + 1)
                then(dve.max(lmax[:, :], bank[7][:, D:D + E]))
                dve.tensor_scalar(ld[:, :], bank[7][:, D:D + E], lmax[:, 0:1], None, ALU.subtract).then_inc(ld_ready, 1)

            def route_middle(g):
                dve.wait_ge(le_ready, g + 1)
                then(dve.max(top[:, :], le[:, :]))
                then(dve.max_index(topi[:, :], top[:, :], le[:, :]))
                then(dve.tensor_copy(topf[:, :], topi[:, 0:K]))
                for k in range(K):
                    then(dve.tensor_scalar(oh[:, k, :], iota8[:, :], topf[:, k:k + 1], None, ALU.is_equal))
                if g >= 1:
                    dve.wait_ge(cum_done, g)
                    then(dve.tensor_tensor(prev[:, :], prev[:, :], sel[:, :], ALU.add))
                dve.tensor_tensor(sel[:, :], oh[:, 0, :], oh[:, 1, :], ALU.add).then_inc(sel_ready, 1)
                then(dve.tensor_tensor(gs[:, 0:1], top[:, 0:1], top[:, 1:2], ALU.add))
                then(dve.reciprocal(gs[:, 1:2], gs[:, 0:1]))
                then(dve.tensor_scalar(gate[:, :], top[:, 0:K], gs[:, 1:2], None, ALU.mult))

            def route_close(g):
                dve.wait_ge(cum_done, g + 1)
                cum = bank[7][:, D + E:D + 2 * E].unsqueeze(1).broadcast_to([P, K, E])
                dve.tensor_tensor(junk[:, :, :], oh[:, :, :], cum, ALU.mult).then_inc(cum_read, 1)
                dve.wait_ge(cum_read, g + 1)
                then(dve.reduce_sum(pos[:, :], junk[:, :, :], AX.X))
                then(dve.tensor_scalar(keep[:, :], pos[:, :], float(CAP), None, ALU.is_lt))
                then(dve.scalar_tensor_tensor(out=dest[:, :], in0=topf[:, :], scalar=float(CAP), in1=pos[:, :],
                                              op0=ALU.mult, op1=ALU.add))
                dve.tensor_tensor(w_sb[:, g, :], gate[:, :], keep[:, :], ALU.mult)
                then(dve.tensor_tensor(dsc[:, 0, :], dest[:, :], trash[:, g, :], ALU.subtract))
                then(dve.tensor_tensor(dsc[:, 0, :], dsc[:, 0, :], keep[:, :], ALU.mult))
                dve.tensor_tensor(send[:, g, :], dsc[:, 0, :], trash[:, g, :], ALU.add).then_inc(send_ready, 1)
                then(dve.tensor_scalar(dsc[:, 1, :], dest[:, :], -float(SLOTS), None, ALU.add))
                then(dve.tensor_tensor(dsc[:, 1, :], dsc[:, 1, :], keep[:, :], ALU.mult))
                then(dve.tensor_scalar(fetch[:, g, :], dsc[:, 1, :], float(SLOTS), None, ALU.add))

            def tick(t):
                a, b, c = t, t - 1, t - 2
                if c >= 0:
                    norms_open(c)
                if 0 <= b < G:
                    softmax_open(b)
                if c >= 0:
                    norms_middle(c)
                if a < G:
                    spread(a)
                if c >= 0:
                    norms_close(c)
                if 0 <= b < G:
                    softmax_close(b)
                if c >= 0:
                    route_open(c)
                if 0 <= b < G:
                    widen(b)
                if c >= 0:
                    route_middle(c)
                    route_close(c)

            for t in range(G + 2):
                tick(t)

            def bias_out(e, r, first):
                for c in range(DC):
                    dve.wait_ge(l2_done, e * DC + c + 1)
                    dve.tensor_scalar(yT[:, r, c, :], bank[4 + c][:, 0:CAP], b2_sb[:, bass.ds(e, 1), c], None,
                                      ALU.add).then_inc(yt_ready, 1)

            def rows_out(e, r, first):
                if not first:
                    for t, (s0, n) in enumerate(YT):
                        dve.wait_ge(yr_done, e * NY + t + 1)
                        dve.tensor_copy(yr[0:n, r, t, :], bank[6 + t % 2][0:n, 0:D]).then_inc(yr_ready, 1)

            def expert(e, r, first):
                if not first:
                    if not isinstance(e, int):
                        dve.wait_ge(stored[1 - r], (e - 1 - (1 - r)) * (8 * NY))
                    rows_out(e - 1, 1 - r, False)
                bias_out(e, r, first)

            dve.wait_ge(small_in, 48)
            expert_loop(dve, expert)
            dve.wait_ge(stored[1], 16 * NY * (E // 2 - 1))
            rows_out(E - 1, 1, False)

            for g in range(G):
                r = g % 2
                dve.wait_ge(fetched[r], 16 * K * (g // 2 + 1))
                if g >= 2:
                    dve.wait_ge(out_done[r], 16 * (g // 2))
                then(dve.scalar_tensor_tensor(out=fin[:, r, :], in0=got[:, r, 0, :], scalar=w_sb[:, g, 0:1],
                                              in1=h_sb[:, g, :], op0=ALU.mult, op1=ALU.add))
                dve.scalar_tensor_tensor(out=fin[:, r, :], in0=got[:, r, 1, :], scalar=w_sb[:, g, 1:2],
                                         in1=fin[:, r, :], op0=ALU.mult, op1=ALU.add).then_inc(fin_ready, 1)

        @block.tensor
        def _(pe):
            pe.wait_ge(made, 13)
            pe.wait_ge(wt_in, 16)

            def embed(g):
                pe.wait_ge(x_in[g], 16)
                if g >= 2:
                    pe.wait_ge(h_ready, g - 1)
                for c in range(IC):
                    mm = pe.matmul(bank[g % 2][:, 0:D], x_sb[:, g, c, :], wt_sb[:, c, :], start=(c == 0), stop=(c == IC - 1))
                mm.then_inc(emb_done, 1)

            def norm_transpose(g):
                pe.wait_ge(xn_ready, g + 1)
                if g >= 2:
                    pe.wait_ge(xnt_ready, g - 1)
                for c in range(DC):
                    mm = pe.transpose(bank[2 + g % 2][:, c * P:(c + 1) * P], xn[:, g % 2, c * P:(c + 1) * P], ident[:, :])
                mm.then_inc(xnt_done, 1)

            for g in range(G + 1):
                if g < G:
                    embed(g)
                if g >= 1:
                    norm_transpose(g - 1)
            pe.wait_ge(wqk_in, 32)
            pe.wait_ge(wvo_in, 32)
            pe.wait_ge(small_in, 48)

            def project(g, w, b, done, read):
                pe.wait_ge(xnt_ready, G if g == 0 else g + 1)
                if g >= 1:
                    pe.wait_ge(read, g)
                elif b < 2:
                    pe.wait_ge(h_ready, G)
                for q in range(QC):
                    for c in range(DC):
                        mm = pe.matmul(bank[b][:, q * P:(q + 1) * P], w[:, c, q * P:(q + 1) * P],
                                       xnT[:, c, g * P:(g + 1) * P], start=(c == 0), stop=(c == DC - 1))
                mm.then_inc(done, 1)

            def project_v(g):
                if g >= 1:
                    pe.wait_ge(v_ready, g)
                for c in range(DC):
                    mm = pe.matmul(bank[2][:, 0:D], xnT[:, c, g * P:(g + 1) * P], wv_sb[:, c, :],
                                   start=(c == 0), stop=(c == DC - 1))
                mm.then_inc(v_done, 1)

            def scores(g):
                pe.wait_ge(kblk_dve, g + 1)
                pe.wait_ge(kblk_pool, g + 1)
                pe.wait_ge(q_ready, g + 1)
                if g >= 1:
                    pe.wait_ge(sd_ready, g)
                for q in range(QC):
                    for i in range(GI):
                        mm = pe.matmul(bank[3][:, q * P + i * S:q * P + (i + 1) * S], kblk[:, q * GI + i, :, :],
                                       qT[:, g % 2, q, i * S:(i + 1) * S], start=True, stop=True)
                mm.then_inc(st_done, 1)

            def score_rows(g):
                pe.wait_ge(st_ready, g + 1)
                for q in range(QC):
                    mm = pe.transpose(bank[3][:, q * P:(q + 1) * P], sT[:, q, :], ident[:, :])
                mm.then_inc(s_done, 1)

            def prob_columns(g):
                pe.wait_ge(pw_dve, g + 1)
                pe.wait_ge(pw_pool, g + 1)
                for n in range(4):
                    m = 4 * g + n
                    if m >= 2:
                        pe.wait_ge(pf_ready, m - 1)
                    for h in range(4):
                        mm = pe.transpose(bank[4 + n % 2][:, h * P:(h + 1) * P], pw[:, 4 * n + h, :, :], ident[:, :])
                    mm.then_inc(pt_done, 1)

            def weigh_values(g):
                pe.wait_ge(pf_ready, 4 * g + 4)
                pe.wait_ge(v_ready, g + 1)
                if g >= 1:
                    pe.wait_ge(wo_read, g)
                for h in range(HEADS):
                    mm = pe.matmul(bank[6][:, h * HD:(h + 1) * HD], pf[:, h, :], v_sb[:, g % 2, h * HD:(h + 1) * HD],
                                   start=True, stop=True)
                mm.then_inc(pv_done, 1)

            def out_project(g):
                pe.wait_ge(o_ready, g + 1)
                for c in range(DC):
                    mm = pe.transpose(bank[6][:, D + c * P:D + (c + 1) * P], o_sb[:, c * P:(c + 1) * P], ident[:, :])
                mm.then_inc(ot_done, 1)
                pe.wait_ge(ot_ready, g + 1)
                for c in range(DC):
                    mm = pe.matmul(bank[6][:, 0:D], oT[:, c, :], wo_sb[:, c, :], start=(c == 0), stop=(c == DC - 1))
                mm.then_inc(wo_done, 1)

            def gate_logits(g):
                pe.wait_ge(x2_ready, g + 1)
                if g >= 1:
                    pe.wait_ge(cum_read, g)
                for c in range(DC):
                    mm = pe.transpose(bank[7][:, c * P:(c + 1) * P], xrow[:, g % 2, c * P:(c + 1) * P], ident[:, :])
                mm.then_inc(x2t_done, 1)
                pe.wait_ge(x2t_ready, g + 1)
                for c in range(DC):
                    mm = pe.matmul(bank[7][:, D:D + E], x2T[:, c, :], wg_sb[:, c, :], start=(c == 0), stop=(c == DC - 1))
                mm.then_inc(lg_done, 1)

            def count(g):
                pe.wait_ge(sel_ready, g + 1)
                pe.matmul(bank[7][:, D + E:D + 2 * E], upper[:, :], sel[:, :], start=True, stop=False)
                pe.matmul(bank[7][:, D + E:D + 2 * E], ones[:, :], prev[:, :], start=False, stop=True).then_inc(cum_done, 1)

            def tick(t):
                a, b, c = t, t - 1, t - 2
                if 0 <= b < G:
                    scores(b)
                if a < G:
                    project(a, wq_sb, 0, q_done, q_ready)
                if 0 <= b < G:
                    score_rows(b)
                if a < G:
                    project(a, wk_sb, 1, k_done, k_ready)
                    project_v(a)
                if c >= 0:
                    gate_logits(c)
                if 0 <= b < G:
                    prob_columns(b)
                    weigh_values(b)
                if c >= 0:
                    count(c)
                if 0 <= b < G:
                    out_project(b)

            for t in range(G + 2):
                tick(t)

            pe.wait_ge(xg_in, 16 * XT)
            for t in range(XT):
                n = min(P, SLOTS - t * P)
                if t >= 4:
                    pe.wait_ge(xt_ready, t - 3)
                for c in range(DC):
                    mm = pe.transpose(bank[t % 4][:, c * n:(c + 1) * n], xg[0:n, t, c * P:(c + 1) * P], ident[0:n, 0:n])
                mm.then_inc(xt_done, 1)
            pe.wait_ge(xt_ready, XT)

            def slot_rows(e, r):
                pe.wait_ge(yt_ready, (e + 1) * DC)
                for t, (s0, n) in enumerate(YT):
                    if t == 2:
                        pe.wait_ge(yr_ready, e * NY + 1)
                    for c in range(DC):
                        mm = pe.transpose(bank[6 + t % 2][0:n, c * P:(c + 1) * P], yT[:, r, c, s0:s0 + n], ident[:, :])
                    mm.then_inc(yr_done, 1)

            def expert(e, r, first):
                pe.wait_ge(w1_in[r], (e - r) * 8 + 16)
                for j in range(HC):
                    if not (first and j < 4):
                        pe.wait_ge(h_done, e * HC + (j - 3))
                    for c in range(DC):
                        mm = pe.matmul(bank[j % 4][:, 0:CAP], w1_sb[:, r, c, j * P:(j + 1) * P],
                                       xT[:, c, bass.ds(e * CAP, CAP)], start=(c == 0), stop=(c == DC - 1))
                    mm.then_inc(l1_done, 1)
                if not first:
                    slot_rows(e - 1, 1 - r)
                pe.wait_ge(w2_in[r], (e - r) * 8 + 16)
                pe.wait_ge(h_done, (e + 1) * HC)
                for c in range(DC):
                    for j in range(HC):
                        mm = pe.matmul(bank[4 + c][:, 0:CAP], w2_sb[:, r, j, c * P:(c + 1) * P], hT[:, r, j, :],
                                       start=(j == 0), stop=(j == HC - 1))
                    mm.then_inc(l2_done, 1)

            expert_loop(pe, expert)
            slot_rows(E - 1, 1)


WDVE = 6
KDVE = 5


def kernel(x, L0_tok_W, L0_tok_b, L0_attn_Wq, L0_attn_Wk, L0_attn_Wv, L0_attn_Wo, L0_attn_lambda_q1,
           L0_attn_lambda_k1, L0_attn_lambda_q2, L0_attn_lambda_k2, L0_attn_gamma, L0_attn_beta,
           L0_ffn_Wg, L0_ffn_W1, L0_ffn_b1, L0_ffn_W2, L0_ffn_b2):
    import concourse.bacc as _bacc
    from concourse.bass_utils import run_bass_kernel_spmd as _run

    def rows_first(w):
        return np.ascontiguousarray(w.reshape(w.shape[0] // P, P, w.shape[1]).transpose(1, 0, 2))

    a = SIDE // PATCH
    img = np.asarray(x).reshape(IMGS, CH, a, PATCH, a, PATCH).transpose(3, 5, 1, 0, 2, 4).reshape(IN, N)
    xh = np.ascontiguousarray(img.reshape(IC, P, G, P).transpose(1, 2, 0, 3))
    n = np.asarray
    ins = {
        "xh": xh,
        "wt": rows_first(n(L0_tok_W).T),
        "tok_b": n(L0_tok_b),
        "wq": rows_first(n(L0_attn_Wq)), "wk": rows_first(n(L0_attn_Wk)),
        "wv": rows_first(n(L0_attn_Wv)), "wo": rows_first(n(L0_attn_Wo)),
        "lam": np.stack([n(L0_attn_lambda_q1), n(L0_attn_lambda_k1), n(L0_attn_lambda_q2),
                         n(L0_attn_lambda_k2)]).reshape(2, 2, HD),
        "gamma": n(L0_attn_gamma), "beta": n(L0_attn_beta),
        "wg": rows_first(n(L0_ffn_Wg)),
        "w1": np.ascontiguousarray(n(L0_ffn_W1).reshape(E, DC, P, HID).transpose(0, 2, 1, 3)),
        "b1": np.ascontiguousarray(n(L0_ffn_b1).reshape(E, HC, P).transpose(2, 0, 1)),
        "w2": np.ascontiguousarray(n(L0_ffn_W2).reshape(E, HC, P, D).transpose(0, 2, 1, 3)),
        "b2": np.ascontiguousarray(n(L0_ffn_b2).reshape(E, DC, P).transpose(2, 0, 1)),
    }
    nc = _bacc.Bacc("TRN2", target_bir_lowering=False, num_devices=1)
    args = [nc.dram_tensor(f"in_{k}", v.shape, F32, kind="ExternalInput").ap() for k, v in ins.items()]
    out = nc.dram_tensor("out", (N, D), F32, kind="ExternalOutput").ap()
    vit_tower(nc, *args, out)
    r = _run(nc, [{f"in_{k}": v for k, v in ins.items()}], core_ids=[0])
    return r.results[0]["out"].reshape(IMGS, S, D)
```

```python
import numpy as np
import concourse.bass as bass
from concourse import mybir
from contextlib import ExitStack
import math

F32 = mybir.dt.float32
U32 = mybir.dt.uint32
BF16 = mybir.dt.bfloat16
ALU = mybir.AluOpType
ACT = mybir.ActivationFunctionType
AX = mybir.AxisListType

P = 128
IMGS, CH, SIDE, PATCH = 64, 3, 64, 16
S = (SIDE // PATCH) ** 2
N = IMGS * S
G = N // P
GI = P // S
D = 256
DC = D // P
IN = PATCH * PATCH * CH
IC = IN // P
HEADS, HD = 16, 16
QC = 2 * D // P
HB = P // HD
NHB = 2 * HEADS
SCALE = HD ** -0.5
LAMBDA_INIT = 0.8 - 0.6 * math.exp(-0.3 * 11)
EPS = 1e-5
E, K, HID = 8, 2, 1024
HC = HID // P
CAP = int(math.ceil(N * K / E * 1.05))
SLOTS = E * CAP
XT = -(-SLOTS // P)
YT = [(t, min(P, CAP - t)) for t in range(0, CAP, P)]
NY = len(YT)


def vit_tower(nc, xh, wt, tok_b, wq, wk, wv, wo, lam, gamma, beta, wg, w1, b1, w2, b2, out):
    ctx = ExitStack()
    with ctx:
        def sb(name, shape, dt=F32):
            return ctx.enter_context(nc.sbuf_tensor(name, shape, dt))

        def sem(name):
            return ctx.enter_context(nc.semaphore(name))

        xbuf = nc.dram_tensor("xbuf", (SLOTS + K * N, D), F32, kind="Internal").ap()
        ybuf = nc.dram_tensor("ybuf", (SLOTS + 1, D), F32, kind="Internal").ap()

        front = sb("front", [P, G * IC * P])
        x_sb = front[:, :].rearrange("p (g c t) -> p g c t", g=G, c=IC)
        xg = front[:, 0:XT * D].rearrange("p (t d) -> p t d", t=XT)
        wt_sb = sb("wt_sb", [P, IC, D])
        wq_sb = sb("wq_sb", [P, DC, 2 * D])
        wk_sb = sb("wk_sb", [P, DC, 2 * D])
        wv_sb = sb("wv_sb", [P, DC, D])
        wo_sb = sb("wo_sb", [P, DC, D])
        wg_sb = sb("wg_sb", [P, DC, E])
        b1_sb = sb("b1_sb", [P, E, HC])
        b2_sb = sb("b2_sb", [P, E, DC])
        rows = sb("rows", [P, 3, D])
        lam_sb = sb("lam_sb", [P, 2, 2, HD])
        lam_pr = sb("lam_pr", [P, 2, HD])
        lam_s = sb("lam_s", [P, 2])
        lam_e = sb("lam_e", [P, 2])
        neglam = sb("neglam", [P, 2])
        ident = sb("ident", [P, P])
        same = sb("same", [P, GI, S])
        upper = sb("upper", [P, P])
        ones = sb("ones", [P, P])
        half = sb("half", [P, 1])
        iota8 = sb("iota8", [P, E])
        trash = sb("trash", [P, G, K])
        zero = sb("zero", [P, D])
        h_sb = sb("h_sb", [P, G, D])
        xn = sb("xn", [P, 2, D])
        xnT = sb("xnT", [P, DC, N])
        q3 = sb("q3", [P, 2, 3, QC, P], BF16)
        k3 = sb("k3", [P, 3, QC * GI, S], BF16)
        q_rest = sb("q_rest", [P, QC * P])
        k_rest = sb("k_rest", [P, QC * P])
        v_sb = sb("v_sb", [P, 2, D])
        big = sb("big", [P, 2 * HC * CAP])
        hT = big[:, :].rearrange("p (r j s) -> p r j s", r=2, j=HC)
        kblk = sb("kblk", [P, 3, QC * GI, HB, S], BF16)
        pf = big[:, 0:HEADS * P].rearrange("p (h t) -> p h t", h=HEADS)
        pw = big[:, HEADS * P:2 * HEADS * P].rearrange("p (h a s) -> p h a s", h=HEADS, a=GI)
        c_sb = sb("c_sb", [P, 2, 2, GI, S])
        bc = sb("bc", [P, 2, 2, GI, S])
        sT = sb("sT", [P, QC, P])
        sd = sb("sd", [P, NHB, S])
        ex = sb("ex", [P, NHB, S])
        prob = sb("prob", [P, HEADS, S])
        o_sb = sb("o_sb", [P, D])
        oT = sb("oT", [P, DC, P])
        t1 = sb("t1", [P, D])
        t2 = sb("t2", [P, D])
        x2T = sb("x2T", [P, DC, P])
        xrow = sb("xrow", [P, 2, D])
        stat = sb("stat", [P, 2, 6])
        mv = sb("mv", [P, 2, 2])
        var = sb("var", [P, 2])
        rstd = sb("rstd", [P, 2])
        stat1 = sb("stat1", [P, 2, 6])
        mv1 = sb("mv1", [P, 2, 2])
        var1 = sb("var1", [P, 2])
        rstd1 = sb("rstd1", [P, 2])
        mx = sb("mx", [P, NHB])
        sm = sb("sm", [P, NHB])
        rc = sb("rc", [P, NHB])
        lmax = sb("lmax", [P, 8])
        ld = sb("ld", [P, E])
        le = sb("le", [P, E])
        top = sb("top", [P, 8])
        topi = sb("topi", [P, 8], U32)
        topf = sb("topf", [P, K])
        oh = sb("oh", [P, K, E])
        sel = sb("sel", [P, E])
        prev = sb("prev", [P, E])
        gs = sb("gs", [P, 2])
        gate = sb("gate", [P, K])
        junk = sb("junk", [P, K, E])
        pos = sb("pos", [P, K])
        keep = sb("keep", [P, K])
        dest = sb("dest", [P, K])
        dsc = sb("dsc", [P, 2, K])
        send = sb("send", [P, G, K], U32)
        fetch = sb("fetch", [P, G, K], U32)
        w_sb = sb("w_sb", [P, G, K])
        w1_sb = sb("w1_sb", [P, 2, DC, HID])
        w2_sb = sb("w2_sb", [P, 2, HC, D])
        xT = sb("xT", [P, DC, SLOTS])
        yT = sb("yT", [P, 2, DC, CAP])
        yr = sb("yr", [P, 2, NY, D])
        got = sb("got", [P, 2, K, D])
        fin = sb("fin", [P, 2, D])

        psum = ctx.enter_context(nc.psum_tensor("psum", [P, 8, 512], F32))
        bank = [psum[:, i, :] for i in range(8)]

        s48 = psum[:, 2:4, 0:3 * P].rearrange("p q (i n s) -> p q i n s", i=GI, n=3)

        x_in = [sem(f"x_in{g}") for g in range(G)]
        wt_in, rows_in, lam_in, wqk_in, wvo_in, small_in = (sem(n) for n in (
            "wt_in", "rows_in", "lam_in", "wqk_in", "wvo_in", "small_in"))
        zeroed = sem("zeroed")
        w1_in = [sem(f"w1_in{i}") for i in range(2)]
        w2_in = [sem(f"w2_in{i}") for i in range(2)]
        xg_in = sem("xg_in")
        made, lam_dve, lam_exp = sem("made"), sem("lam_dve"), sem("lam_exp")
        step = sem("step")
        emb_done, h_ready, ln1_var, ln1_rstd, xn_ready, xnt_done, xnt_ready = (sem(n) for n in (
            "emb_done", "h_ready", "ln1_var", "ln1_rstd", "xn_ready", "xnt_done", "xnt_ready"))
        q_done, k_done, v_done, q_hi, k_hi, q_res, k_res, q_mid, k_mid, q_lo, k_lo, v_ready, kblk_dve, kblk_pool = (
            sem(n) for n in ("q_done", "k_done", "v_done", "q_hi", "k_hi", "q_res", "k_res", "q_mid", "k_mid",
                             "q_lo", "k_lo", "v_ready", "kblk_dve", "kblk_pool"))
        st_done, c_ready, st_ready, s_done, sd_ready, ex_ready, p_ready, pt_done, pf_ready, pv_done = (sem(n) for n in (
            "st_done", "c_ready", "st_ready", "s_done", "sd_ready", "ex_ready", "p_ready", "pt_done", "pf_ready", "pv_done"))
        pw_act, pw_pool = sem("pw_act"), sem("pw_pool")
        o_ready, ot_done, ot_ready, wo_done, wo_read = (sem(n) for n in (
            "o_ready", "ot_done", "ot_ready", "wo_done", "wo_read"))
        lno_var, lno_rstd, ln2_var, ln2_rstd, x2_ready, x2t_done, x2t_ready, lg_done, ld_ready, le_ready = (
            sem(n) for n in ("lno_var", "lno_rstd", "ln2_var", "ln2_rstd", "x2_ready", "x2t_done",
                             "x2t_ready", "lg_done", "ld_ready", "le_ready"))
        sel_ready, prev_ready, cum_done, cum_read, send_ready = (sem(n) for n in (
            "sel_ready", "prev_ready", "cum_done", "cum_read", "send_ready"))
        sent = [sem(f"sent{i}") for i in range(2)]
        xt_done, xt_ready, l1_done, h_done, l2_done, yt_ready, yr_done, yr_ready = (sem(n) for n in (
            "xt_done", "xt_ready", "l1_done", "h_done", "l2_done", "yt_ready", "yr_done", "yr_ready"))
        stored = [sem(f"stored{i}") for i in range(2)]
        fetched = [sem(f"fetched{i}") for i in range(2)]
        fin_ready = sem("fin_ready")
        out_done = [sem(f"out_done{i}") for i in range(2)]

        block = ctx.enter_context(nc.Block())

        def expert_loop(eng, body):
            for r in range(2):
                body(r, r, r == 0)
            with eng.Fori(1, E // 2) as i:
                for r in range(2):
                    body(i * 2 + r, r, False)

        @block.sync
        def _(sp):
            sp.dma_start(x_sb[:, 0, :, :], xh[:, 0, :, :]).then_inc(x_in[0], 16)
            sp.dma_start(wt_sb[:, :, :], wt).then_inc(wt_in, 16)
            for n, r in enumerate((tok_b, gamma, beta)):
                sp.dma_start(rows[:, n, :], r.partition_broadcast(P)).then_inc(rows_in, 16)
            for g in range(1, G):
                sp.dma_start(x_sb[:, g, :, :], xh[:, g, :, :]).then_inc(x_in[g], 16)
            sp.dma_start(wq_sb[:, :, :], wq).then_inc(wqk_in, 16)
            sp.dma_start(wk_sb[:, :, :], wk).then_inc(wqk_in, 16)
            sp.dma_start(wv_sb[:, :, :], wv).then_inc(wvo_in, 16)
            sp.dma_start(wo_sb[:, :, :], wo).then_inc(wvo_in, 16)
            sp.dma_start(lam_sb[:, :, :, :], lam.partition_broadcast(P)).then_inc(lam_in, 16)
            for t, s in ((wg_sb, wg), (b1_sb, b1), (b2_sb, b2)):
                sp.dma_start(t[:, :, :], s).then_inc(small_in, 16)
            sp.wait_ge(made, 1)
            for t in range(XT):
                n = min(P, SLOTS - t * P)
                sp.dma_start(xbuf[t * P:t * P + n, :], zero[0:n, :]).then_inc(zeroed, 16)
            sp.dma_start(ybuf[SLOTS:SLOTS + 1, :], zero[0:1, :]).then_inc(zeroed, 16)
            for e in range(2):
                sp.dma_start(w1_sb[:, e, :, :], w1[e, :, :, :]).then_inc(w1_in[e], 16)
                sp.dma_start(w2_sb[:, e, :, :], w2[e, :, :, :]).then_inc(w2_in[e], 16)
            for r in range(2):
                sp.wait_ge(sent[r], 16 * K * (G // 2))
            for t in range(XT):
                n = min(P, SLOTS - t * P)
                sp.dma_start(xg[0:n, t, :], xbuf[t * P:t * P + n, :]).then_inc(xg_in, 16)

            def stage(e, r, first):
                sp.wait_ge(l2_done, (e + 1) * DC)
                sp.dma_start(w1_sb[:, r, :, :], w1[e + 2, :, :, :]).then_inc(w1_in[r], 16)
                sp.dma_start(w2_sb[:, r, :, :], w2[e + 2, :, :, :]).then_inc(w2_in[r], 16)
                store(e, r)

            def store(e, r):
                sp.wait_ge(yr_ready, (e + 1) * NY)
                for t, (s0, n) in enumerate(YT):
                    sp.dma_start(ybuf[bass.ds(e * CAP + s0, n), :], yr[0:n, r, t, :]).then_inc(stored[r], 16)

            for r in range(2):
                stage(r, r, False)
            with sp.Fori(1, E // 2 - 1) as i:
                for r in range(2):
                    stage(i * 2 + r, r, False)
            for e in (E - 2, E - 1):
                store(e, e % 2)
            for g in range(G):
                sp.wait_ge(fin_ready, g + 1)
                sp.dma_start(out[g * P:(g + 1) * P, :], fin[:, g % 2, :]).then_inc(out_done[g % 2], 16)
            for r in range(2):
                sp.wait_ge(out_done[r], 16 * (G // 2))

        @block.gpsimd
        def _(pool):
            pool.memset(zero[:, :], 0.0).then_inc(made, 1)
            pool.memset(ident[:, :], 0.0).then_inc(made, 1)
            pool.memset(same[:, :, :], 1.0).then_inc(made, 1)
            pool.memset(upper[:, :], 1.0).then_inc(made, 1)
            pool.memset(ones[:, :], 1.0).then_inc(made, 1)
            pool.memset(half[:, :], -0.5).then_inc(made, 1)
            pool.memset(prev[:, :], 0.0).then_inc(made, 1)
            pool.iota(iota8[:, :], pattern=[[1, E]], base=0, channel_multiplier=0,
                      allow_small_or_imprecise_dtypes=True).then_inc(made, 1)
            pool.iota(trash[:, :, :], pattern=[[K * P, G], [P, K]], base=SLOTS, channel_multiplier=1,
                      allow_small_or_imprecise_dtypes=True).then_inc(made, 1)
            pool.wait_ge(made, 9)
            pool.affine_select(out=ident[:, :], in_=ident[:, :], compare_op=ALU.not_equal, fill=1.0, base=0,
                               pattern=[[-1, P]], channel_multiplier=1).then_inc(made, 1)
            pool.affine_select(out=same[:, :, :], in_=same[:, :, :], compare_op=ALU.is_ge, fill=0.0, base=0,
                               pattern=[[-S, GI], [0, S]], channel_multiplier=1).then_inc(made, 1)
            pool.wait_ge(made, 11)
            pool.affine_select(out=same[:, :, :], in_=same[:, :, :], compare_op=ALU.is_ge, fill=0.0, base=S - 1,
                               pattern=[[S, GI], [0, S]], channel_multiplier=-1).then_inc(made, 1)
            pool.affine_select(out=upper[:, :], in_=upper[:, :], compare_op=ALU.is_gt, fill=0.0, base=0,
                               pattern=[[1, P]], channel_multiplier=-1).then_inc(made, 1)
            pool.wait_ge(made, 13)

            def power(var_sem, rstd_sem, src, dst, g):
                pool.wait_ge(var_sem, g + 1)
                pool.tensor_tensor(dst, src, half[:, :], ALU.pow).then_inc(rstd_sem, 1)

            for g in range(G):
                power(ln1_var, ln1_rstd, var1[:, g % 2:g % 2 + 1], rstd1[:, g % 2:g % 2 + 1], g)

            def tick(t):
                a, b, c, d = t, t - 1, t - 2, t - 3
                if d >= 0:
                    power(lno_var, lno_rstd, var[:, 0:1], rstd[:, 0:1], d)
                if a < G:
                    pool.wait_ge(k_mid, a + 1)
                    pool.tensor_tensor(k3[:, 2, :, :], k_rest[:, :], k3[:, 1, :, :], ALU.subtract).then_inc(k_lo, 1)
                if d >= 0:
                    power(ln2_var, ln2_rstd, var[:, 1:2], rstd[:, 1:2], d)
                if a < G:
                    pool.wait_ge(k_lo, a + 1)
                    if b >= 0:
                        pool.wait_ge(st_done, 2 * b + 2)
                    for j in range(KDVE, HB):
                        ins = pool.tensor_scalar(kblk[:, :, :, j, :], k3[:, :, :, :], same[:, j, 0:1], 1.0,
                                                 ALU.mult, ALU.mult)
                    ins.then_inc(kblk_pool, 1)
                if a < G:
                    pool.wait_ge(q_mid, a + 1)
                    pool.tensor_tensor(q3[:, a % 2, 2, :, :], q_rest[:, :], q3[:, a % 2, 1, :, :],
                                       ALU.subtract).then_inc(q_lo, 1)
                if 0 <= b < G and WACT < GI:
                    pool.wait_ge(p_ready, b + 1)
                    if b >= 1:
                        pool.wait_ge(pt_done, 4 * b)
                    for i in range(WACT, GI):
                        ins = pool.tensor_scalar(pw[:, :, i, :], prob[:, :, :], same[:, i, 0:1], 1.0, ALU.mult, ALU.mult)
                    ins.then_inc(pw_pool, 1)
                if d >= 0:
                    if d == 0:
                        pool.wait_ge(zeroed, 16 * (XT + 1))
                    pool.wait_ge(send_ready, d + 1)
                    for k in range(K):
                        pool.indirect_dma_start(
                            out=xbuf[:, :], out_offset=bass.IndirectOffsetOnAxis(ap=send[:, d, k:k + 1], axis=0),
                            in_=xrow[:, d % 2, :], in_offset=None).then_inc(sent[d % 2], 16)

            for t in range(G + 3):
                tick(t)
            for r in range(2):
                pool.wait_ge(stored[r], 16 * NY * (E // 2))
            for g in range(G):
                if g >= 2:
                    pool.wait_ge(fin_ready, g - 1)
                for k in range(K):
                    pool.indirect_dma_start(
                        out=got[:, g % 2, k, :], out_offset=None, in_=ybuf[:, :],
                        in_offset=bass.IndirectOffsetOnAxis(ap=fetch[:, g, k:k + 1], axis=0)).then_inc(fetched[g % 2], 16)

        @block.scalar
        def _(act):
            for g in range(G):
                act.wait_ge(xnt_done, g + 1)
                act.activation(xnT[:, :, g * P:(g + 1) * P],
                               bank[2 + g % 2][:, 0:D].rearrange("p (c t) -> p c t", c=DC), ACT.Copy).then_inc(xnt_ready, 1)

            act.wait_ge(lam_dve, 1)
            act.activation(lam_e[:, :], lam_s[:, :], ACT.Exp).then_inc(lam_exp, 1)

            def third(b, h):
                act.wait_ge(st_done, 2 * b + h + 1)
                if b >= 1:
                    act.wait_ge(st_ready, 2 * b + h - 1)
                act.activation(c_sb[:, h, :, :, :], s48[:, :, :, 2, :], ACT.Copy).then_inc(c_ready, 1)

            def prob_out(c, n):
                act.wait_ge(pt_done, 4 * c + n + 1)
                if n == 0 and c >= 1:
                    act.wait_ge(pv_done, c)
                act.activation(pf[:, 4 * n:4 * n + 4, :], bank[4 + n % 2][:, :], ACT.Copy).then_inc(pf_ready, 1)

            def tick(t):
                a, b, c, d = t, t - 1, t - 2, t - 3
                if 0 <= b < G:
                    third(b, 0)
                if a < G:
                    act.wait_ge(k_done, a + 1)
                    if a >= 1:
                        act.wait_ge(kblk_dve, a)
                        act.wait_ge(kblk_pool, a)
                    act.activation(k3[:, 0, :, :], bank[0][:, :], ACT.Copy).then_inc(k_hi, 1)
                if 0 <= c < G:
                    prob_out(c, 0)
                    prob_out(c, 1)
                if a < G:
                    act.wait_ge(k_res, a + 1)
                    act.activation(k3[:, 1, :, :], k_rest[:, :], ACT.Copy).then_inc(k_mid, 1)
                if 0 <= b < G:
                    third(b, 1)
                if 0 <= c < G:
                    prob_out(c, 2)
                    prob_out(c, 3)
                if a < G:
                    act.wait_ge(q_done, a + 1)
                    if a >= 2:
                        act.wait_ge(st_done, 2 * (a - 1))
                    act.activation(q3[:, a % 2, 0, :, :], bank[1][:, :], ACT.Copy).then_inc(q_hi, 1)
                    act.wait_ge(q_res, a + 1)
                    act.activation(q3[:, a % 2, 1, :, :], q_rest[:, :], ACT.Copy).then_inc(q_mid, 1)
                if d >= 0:
                    act.wait_ge(x2t_done, d + 1)
                    act.activation(x2T[:, :, :], bank[7][:, 0:D], ACT.Copy).then_inc(x2t_ready, 1)
                    act.wait_ge(ld_ready, d + 1)
                    act.activation(le[:, :], ld[:, :], ACT.Exp).then_inc(le_ready, 1)
                if 0 <= b < G:
                    act.wait_ge(sd_ready, b + 1)
                    act.activation(ex[:, :, :], sd[:, :, :], ACT.Exp, scale=SCALE).then_inc(ex_ready, 1)
                if 0 <= c < G:
                    act.wait_ge(pv_done, c + 1)
                    act.activation(o_sb[:, :], bank[6][:, 0:D], ACT.Copy).then_inc(o_ready, 1)
                if a < G:
                    act.wait_ge(v_done, a + 1)
                    if a >= 2:
                        act.wait_ge(pv_done, a - 1)
                    act.activation(v_sb[:, a % 2, :], bank[1][:, 0:D], ACT.Copy).then_inc(v_ready, 1)
                if 0 <= c < G:
                    act.wait_ge(ot_done, c + 1)
                    act.activation(oT[:, :, :], bank[6][:, D:2 * D], ACT.Copy).then_inc(ot_ready, 1)
                if 0 <= b < G:
                    act.wait_ge(p_ready, b + 1)
                    if b >= 1:
                        act.wait_ge(pt_done, 4 * b)
                    for i in range(WACT):
                        ins = act.activation(pw[:, :, i, :], prob[:, :, :], ACT.Copy, scale=same[:, i, 0:1])
                    ins.then_inc(pw_act, 1)

            for t in range(G + 3):
                tick(t)
            for t in range(XT):
                n = min(P, SLOTS - t * P)
                act.wait_ge(xt_done, t + 1)
                act.activation(xT[:, :, t * P:t * P + n],
                               bank[t % 4][:, 0:DC * n].rearrange("p (c s) -> p c s", c=DC), ACT.Copy).then_inc(xt_ready, 1)

            def expert(e, r, first):
                for j in range(HC):
                    act.wait_ge(l1_done, e * HC + j + 1)
                    act.activation(hT[:, r, j, :], bank[j % 4][:, 0:CAP], ACT.Gelu_apprx_tanh,
                                   bias=b1_sb[:, bass.ds(e, 1), j]).then_inc(h_done, 1)

            act.wait_ge(small_in, 48)
            act.wait_ge(xt_ready, XT)
            expert_loop(act, expert)

        @block.vector
        def _(dve):
            steps = [0]

            def then(ins):
                steps[0] += 1
                ins.then_inc(step, 1)
                dve.wait_ge(step, steps[0])

            dve.wait_ge(rows_in, 48)

            def embed_open(g):
                r = g % 2
                dve.wait_ge(emb_done, g + 1)
                dve.tensor_tensor(h_sb[:, g, :], bank[r][:, 0:D], rows[:, 0, :], ALU.add).then_inc(h_ready, 1)
                dve.wait_ge(h_ready, g + 1)
                then(dve.bn_stats(stat1[:, r, :], h_sb[:, g, :]))
                then(dve.bn_aggr(mv1[:, r, :], stat1[:, r, :]))
                dve.tensor_scalar(var1[:, r:r + 1], mv1[:, r, 1:2], EPS, None, ALU.add).then_inc(ln1_var, 1)

            def embed_close(g):
                r = g % 2
                dve.wait_ge(ln1_rstd, g + 1)
                if g >= 2:
                    dve.wait_ge(xnt_done, g - 1)
                dve.tensor_scalar(xn[:, r, :], h_sb[:, g, :], mv1[:, r, 0:1], rstd1[:, r:r + 1],
                                  ALU.subtract, ALU.mult).then_inc(xn_ready, 1)
                then(dve.tensor_tensor(h_sb[:, g, :], h_sb[:, g, :], rows[:, 2, :], ALU.add))

            for g in range(G + 1):
                if g < G:
                    embed_open(g)
                if g >= 1:
                    embed_close(g - 1)
            dve.wait_ge(lam_in, 16)
            then(dve.tensor_tensor(lam_pr[:, :, :], lam_sb[:, :, 0, :], lam_sb[:, :, 1, :], ALU.mult))
            dve.reduce_sum(lam_s[:, :], lam_pr[:, :, :], AX.X).then_inc(lam_dve, 1)
            dve.wait_ge(lam_exp, 1)
            then(dve.tensor_tensor(neglam[:, 0:1], lam_e[:, 1:2], lam_e[:, 0:1], ALU.subtract))
            then(dve.tensor_scalar(neglam[:, 1:2], neglam[:, 0:1], -LAMBDA_INIT, None, ALU.add))
            dve.wait_ge(made, 13)

            def softmax_open(g):
                s3 = bank[2][:, :].rearrange("p (a s) -> p a s", s=S)
                dve.wait_ge(s_done, g + 1)
                then(dve.reduce_max(mx[:, :], s3, AX.X))
                dve.tensor_tensor(sd[:, :, :], s3, mx[:, :].unsqueeze(2).broadcast_to([P, NHB, S]),
                                  ALU.subtract).then_inc(sd_ready, 1)

            def rest(g, b, hi, first, res, lo, out):
                dve.wait_ge(hi, g + 1)
                if g >= 1:
                    dve.wait_ge(lo, g)
                dve.tensor_tensor(out[:, :], bank[b][:, :], first, ALU.subtract).then_inc(res, 1)

            def add_scores(g, h):
                dve.wait_ge(c_ready, 2 * g + h + 1)
                then(dve.tensor_tensor(bc[:, h, :, :, :], s48[:, :, :, 1, :], c_sb[:, h, :, :, :], ALU.add))
                if g >= 1:
                    dve.wait_ge(s_done, g)
                dve.tensor_tensor(sT[:, 2 * h:2 * h + 2, :].rearrange("p q (i s) -> p q i s", i=GI), s48[:, :, :, 0, :],
                                  bc[:, h, :, :, :], ALU.add).then_inc(st_ready, 1)

            def spread(g):
                dve.wait_ge(k_lo, g + 1)
                if g >= 1:
                    dve.wait_ge(st_done, 2 * g)
                for j in range(KDVE):
                    ins = dve.tensor_scalar(kblk[:, :, :, j, :], k3[:, :, :, :], same[:, j, 0:1], None, ALU.mult)
                ins.then_inc(kblk_dve, 1)

            def softmax_close(g):
                dve.wait_ge(ex_ready, g + 1)
                then(dve.reduce_sum(sm[:, :], ex[:, :, :], AX.X))
                then(dve.reciprocal(rc[:, :], sm[:, :]))
                second = rc[:, :].rearrange("p (h b) -> p h b", b=2)[:, :, 1]
                then(dve.tensor_scalar(second, second, neglam[:, 1:2], None, ALU.mult))
                then(dve.tensor_tensor(ex[:, :, :], ex[:, :, :], rc[:, :].unsqueeze(2).broadcast_to([P, NHB, S]), ALU.mult))
                if g >= 1:
                    dve.wait_ge(pw_act, g)
                    dve.wait_ge(pw_pool, g)
                pair = ex[:, :, :].rearrange("p (h b) s -> p h b s", b=2)
                dve.tensor_tensor(prob[:, :, :], pair[:, :, 0, :], pair[:, :, 1, :], ALU.add).then_inc(p_ready, 1)

            def norms_open(g):
                dve.wait_ge(wo_done, g + 1)
                then(dve.bn_stats(stat[:, 0, :], bank[6][:, 0:D]))
                then(dve.bn_aggr(mv[:, 0, :], stat[:, 0, :]))
                dve.tensor_scalar(var[:, 0:1], mv[:, 0, 1:2], EPS, None, ALU.add).then_inc(lno_var, 1)

            def norms_middle(g):
                dve.wait_ge(lno_rstd, g + 1)
                dve.tensor_scalar(t1[:, :], bank[6][:, 0:D], mv[:, 0, 0:1], rstd[:, 0:1],
                                  ALU.subtract, ALU.mult).then_inc(wo_read, 1)
                dve.wait_ge(wo_read, g + 1)
                then(dve.tensor_tensor(t2[:, :], t1[:, :], rows[:, 1, :], ALU.mult))
                then(dve.tensor_tensor(h_sb[:, g, :], t2[:, :], h_sb[:, g, :], ALU.add))
                then(dve.bn_stats(stat[:, 1, :], h_sb[:, g, :]))
                then(dve.bn_aggr(mv[:, 1, :], stat[:, 1, :]))
                dve.tensor_scalar(var[:, 1:2], mv[:, 1, 1:2], EPS, None, ALU.add).then_inc(ln2_var, 1)

            def norms_close(g):
                dve.wait_ge(ln2_rstd, g + 1)
                if g >= 2:
                    dve.wait_ge(sent[g % 2], 16 * K * (g // 2))
                dve.tensor_scalar(xrow[:, g % 2, :], h_sb[:, g, :], mv[:, 1, 0:1], rstd[:, 1:2],
                                  ALU.subtract, ALU.mult).then_inc(x2_ready, 1)

            def route_open(g):
                dve.wait_ge(lg_done, g + 1)
                then(dve.max(lmax[:, :], bank[7][:, D:D + E]))
                dve.tensor_scalar(ld[:, :], bank[7][:, D:D + E], lmax[:, 0:1], None, ALU.subtract).then_inc(ld_ready, 1)

            def route_middle(g):
                dve.wait_ge(le_ready, g + 1)
                then(dve.max(top[:, :], le[:, :]))
                then(dve.max_index(topi[:, :], top[:, :], le[:, :]))
                then(dve.tensor_copy(topf[:, :], topi[:, 0:K]))
                for k in range(K):
                    then(dve.tensor_scalar(oh[:, k, :], iota8[:, :], topf[:, k:k + 1], None, ALU.is_equal))
                if g >= 1:
                    dve.wait_ge(cum_done, g)
                    then(dve.tensor_tensor(prev[:, :], prev[:, :], sel[:, :], ALU.add))
                dve.tensor_tensor(sel[:, :], oh[:, 0, :], oh[:, 1, :], ALU.add).then_inc(sel_ready, 1)
                then(dve.tensor_tensor(gs[:, 0:1], top[:, 0:1], top[:, 1:2], ALU.add))
                then(dve.reciprocal(gs[:, 1:2], gs[:, 0:1]))
                then(dve.tensor_scalar(gate[:, :], top[:, 0:K], gs[:, 1:2], None, ALU.mult))

            def route_close(g):
                dve.wait_ge(cum_done, g + 1)
                cum = bank[7][:, D + E:D + 2 * E].unsqueeze(1).broadcast_to([P, K, E])
                dve.tensor_tensor(junk[:, :, :], oh[:, :, :], cum, ALU.mult).then_inc(cum_read, 1)
                dve.wait_ge(cum_read, g + 1)
                then(dve.reduce_sum(pos[:, :], junk[:, :, :], AX.X))
                then(dve.tensor_scalar(keep[:, :], pos[:, :], float(CAP), None, ALU.is_lt))
                then(dve.scalar_tensor_tensor(out=dest[:, :], in0=topf[:, :], scalar=float(CAP), in1=pos[:, :],
                                              op0=ALU.mult, op1=ALU.add))
                dve.tensor_tensor(w_sb[:, g, :], gate[:, :], keep[:, :], ALU.mult)
                then(dve.tensor_tensor(dsc[:, 0, :], dest[:, :], trash[:, g, :], ALU.subtract))
                then(dve.tensor_tensor(dsc[:, 0, :], dsc[:, 0, :], keep[:, :], ALU.mult))
                dve.tensor_tensor(send[:, g, :], dsc[:, 0, :], trash[:, g, :], ALU.add).then_inc(send_ready, 1)
                then(dve.tensor_scalar(dsc[:, 1, :], dest[:, :], -float(SLOTS), None, ALU.add))
                then(dve.tensor_tensor(dsc[:, 1, :], dsc[:, 1, :], keep[:, :], ALU.mult))
                then(dve.tensor_scalar(fetch[:, g, :], dsc[:, 1, :], float(SLOTS), None, ALU.add))

            def tick(t):
                a, b, d = t, t - 1, t - 3
                if d >= 0:
                    norms_open(d)
                if 0 <= b < G:
                    add_scores(b, 0)
                if a < G:
                    rest(a, 0, k_hi, k3[:, 0, :, :].rearrange("p a s -> p (a s)"), k_res, k_lo, k_rest)
                if d >= 0:
                    norms_middle(d)
                if 0 <= b < G:
                    add_scores(b, 1)
                if d >= 0:
                    norms_close(d)
                if a < G:
                    rest(a, 1, q_hi, q3[:, a % 2, 0, :, :].rearrange("p q t -> p (q t)"), q_res, q_lo, q_rest)
                if d >= 0:
                    route_open(d)
                if 0 <= b < G:
                    softmax_open(b)
                if d >= 0:
                    route_middle(d)
                if a < G:
                    spread(a)
                if 0 <= b < G:
                    softmax_close(b)
                if d >= 0:
                    route_close(d)

            for t in range(G + 3):
                tick(t)

            def bias_out(e, r, first):
                for c in range(DC):
                    dve.wait_ge(l2_done, e * DC + c + 1)
                    dve.tensor_scalar(yT[:, r, c, :], bank[4 + c][:, 0:CAP], b2_sb[:, bass.ds(e, 1), c], None,
                                      ALU.add).then_inc(yt_ready, 1)

            def rows_out(e, r, first):
                if not first:
                    for t, (s0, n) in enumerate(YT):
                        dve.wait_ge(yr_done, e * NY + t + 1)
                        dve.tensor_copy(yr[0:n, r, t, :], bank[6 + t % 2][0:n, 0:D]).then_inc(yr_ready, 1)

            def expert(e, r, first):
                if not first:
                    if not isinstance(e, int):
                        dve.wait_ge(stored[1 - r], (e - 1 - (1 - r)) * (8 * NY))
                    rows_out(e - 1, 1 - r, False)
                bias_out(e, r, first)

            dve.wait_ge(small_in, 48)
            expert_loop(dve, expert)
            dve.wait_ge(stored[1], 16 * NY * (E // 2 - 1))
            rows_out(E - 1, 1, False)

            for g in range(G):
                r = g % 2
                dve.wait_ge(fetched[r], 16 * K * (g // 2 + 1))
                if g >= 2:
                    dve.wait_ge(out_done[r], 16 * (g // 2))
                then(dve.scalar_tensor_tensor(out=fin[:, r, :], in0=got[:, r, 0, :], scalar=w_sb[:, g, 0:1],
                                              in1=h_sb[:, g, :], op0=ALU.mult, op1=ALU.add))
                dve.scalar_tensor_tensor(out=fin[:, r, :], in0=got[:, r, 1, :], scalar=w_sb[:, g, 1:2],
                                         in1=fin[:, r, :], op0=ALU.mult, op1=ALU.add).then_inc(fin_ready, 1)

        @block.tensor
        def _(pe):
            pe.wait_ge(wt_in, 16)
            pe.wait_ge(made, 13)

            def embed(g):
                pe.wait_ge(x_in[g], 16)
                if g >= 2:
                    pe.wait_ge(h_ready, g - 1)
                for c in range(IC):
                    mm = pe.matmul(bank[g % 2][:, 0:D], x_sb[:, g, c, :], wt_sb[:, c, :], start=(c == 0), stop=(c == IC - 1))
                mm.then_inc(emb_done, 1)

            def norm_transpose(g):
                pe.wait_ge(xn_ready, g + 1)
                if g >= 2:
                    pe.wait_ge(xnt_ready, g - 1)
                for c in range(DC):
                    mm = pe.transpose(bank[2 + g % 2][:, c * P:(c + 1) * P], xn[:, g % 2, c * P:(c + 1) * P], ident[:, :])
                mm.then_inc(xnt_done, 1)

            for g in range(G + 2):
                if g < G:
                    embed(g)
                if g >= 2:
                    norm_transpose(g - 2)
            pe.wait_ge(wqk_in, 32)
            pe.wait_ge(wvo_in, 32)
            pe.wait_ge(small_in, 48)

            def project(g, w, b, done, read):
                pe.wait_ge(xnt_ready, G if g == 0 else g + 1)
                if g >= 1:
                    pe.wait_ge(read, g)
                else:
                    pe.wait_ge(h_ready, G)
                for q in range(QC):
                    for c in range(DC):
                        mm = pe.matmul(bank[b][:, q * P:(q + 1) * P], w[:, c, q * P:(q + 1) * P],
                                       xnT[:, c, g * P:(g + 1) * P], start=(c == 0), stop=(c == DC - 1))
                mm.then_inc(done, 1)

            def project_v(g):
                pe.wait_ge(q_res, g + 1)
                for c in range(DC):
                    mm = pe.matmul(bank[1][:, 0:D], xnT[:, c, g * P:(g + 1) * P], wv_sb[:, c, :],
                                   start=(c == 0), stop=(c == DC - 1))
                mm.then_inc(v_done, 1)

            def scores(g, h):
                if h == 0:
                    pe.wait_ge(kblk_dve, g + 1)
                    pe.wait_ge(kblk_pool, g + 1)
                    pe.wait_ge(q_lo, g + 1)
                    if g >= 1:
                        pe.wait_ge(sd_ready, g)
                else:
                    pe.wait_ge(st_ready, 2 * g + 1)
                for q in range(2):
                    for i in range(GI):
                        for n in range(3):
                            mm = pe.matmul(s48[:, q, i, n:3, :], kblk[:, n, (2 * h + q) * GI + i, :, :],
                                           q3[:, g % 2, 0:3 - n, 2 * h + q, i * S:(i + 1) * S],
                                           start=(n == 0), stop=(n == 2))
                mm.then_inc(st_done, 1)

            def score_rows(g):
                pe.wait_ge(st_ready, 2 * g + 2)
                for q in range(QC):
                    mm = pe.transpose(bank[2][:, q * P:(q + 1) * P], sT[:, q, :], ident[:, :])
                mm.then_inc(s_done, 1)

            def prob_columns(g, n):
                if n == 0:
                    pe.wait_ge(pw_act, g + 1)
                    pe.wait_ge(pw_pool, g + 1)
                m = 4 * g + n
                if m >= 2:
                    pe.wait_ge(pf_ready, m - 1)
                for h in range(4):
                    mm = pe.transpose(bank[4 + n % 2][:, h * P:(h + 1) * P], pw[:, 4 * n + h, :, :], ident[:, :])
                mm.then_inc(pt_done, 1)

            def weigh_values(g, later):
                pe.wait_ge(pf_ready, 4 * g + 4)
                pe.wait_ge(v_ready, g + 1)
                if g >= 1:
                    pe.wait_ge(wo_read, g)
                for h in range(HEADS):
                    mm = pe.matmul(bank[6][:, h * HD:(h + 1) * HD], pf[:, h, :], v_sb[:, g % 2, h * HD:(h + 1) * HD],
                                   start=True, stop=True)
                    if h == 4:
                        later()
                mm.then_inc(pv_done, 1)

            def out_project(g):
                pe.wait_ge(o_ready, g + 1)
                for c in range(DC):
                    mm = pe.transpose(bank[6][:, D + c * P:D + (c + 1) * P], o_sb[:, c * P:(c + 1) * P], ident[:, :])
                mm.then_inc(ot_done, 1)

            def out_project_close(g):
                pe.wait_ge(ot_ready, g + 1)
                for c in range(DC):
                    mm = pe.matmul(bank[6][:, 0:D], oT[:, c, :], wo_sb[:, c, :], start=(c == 0), stop=(c == DC - 1))
                mm.then_inc(wo_done, 1)

            def gate_logits(g):
                pe.wait_ge(x2_ready, g + 1)
                if g >= 1:
                    pe.wait_ge(cum_read, g)
                for c in range(DC):
                    mm = pe.transpose(bank[7][:, c * P:(c + 1) * P], xrow[:, g % 2, c * P:(c + 1) * P], ident[:, :])
                mm.then_inc(x2t_done, 1)

            def gate_logits_close(g):
                pe.wait_ge(x2t_ready, g + 1)
                for c in range(DC):
                    mm = pe.matmul(bank[7][:, D:D + E], x2T[:, c, :], wg_sb[:, c, :], start=(c == 0), stop=(c == DC - 1))
                mm.then_inc(lg_done, 1)

            def count(g):
                pe.wait_ge(sel_ready, g + 1)
                pe.matmul(bank[7][:, D + E:D + 2 * E], upper[:, :], sel[:, :], start=True, stop=False)
                pe.matmul(bank[7][:, D + E:D + 2 * E], ones[:, :], prev[:, :], start=False, stop=True).then_inc(cum_done, 1)

            def tick(t):
                a, b, c, d = t, t - 1, t - 2, t - 3
                if 0 <= b < G:
                    scores(b, 0)
                if a < G:
                    project(a, wk_sb, 0, k_done, k_res)
                if 0 <= c < G:
                    prob_columns(c, 0)
                    prob_columns(c, 1)
                if 0 <= b < G:
                    scores(b, 1)
                if 0 <= c < G:
                    prob_columns(c, 2)
                    prob_columns(c, 3)
                if a < G:
                    project(a, wq_sb, 1, q_done, v_ready)
                if d >= 0:
                    gate_logits(d)

                def later():
                    if d >= 0:
                        gate_logits_close(d)
                    if 0 <= b < G:
                        score_rows(b)

                if 0 <= c < G:
                    weigh_values(c, later)
                else:
                    later()
                if a < G:
                    project_v(a)
                if 0 <= c < G:
                    out_project(c)
                if d >= 0:
                    count(d)
                if 0 <= c < G:
                    out_project_close(c)

            for t in range(G + 3):
                tick(t)

            pe.wait_ge(xg_in, 16 * XT)
            for t in range(XT):
                n = min(P, SLOTS - t * P)
                if t >= 4:
                    pe.wait_ge(xt_ready, t - 3)
                for c in range(DC):
                    mm = pe.transpose(bank[t % 4][:, c * n:(c + 1) * n], xg[0:n, t, c * P:(c + 1) * P], ident[0:n, 0:n])
                mm.then_inc(xt_done, 1)
            pe.wait_ge(xt_ready, XT)

            def slot_rows(e, r):
                pe.wait_ge(yt_ready, (e + 1) * DC)
                for t, (s0, n) in enumerate(YT):
                    if t == 2:
                        pe.wait_ge(yr_ready, e * NY + 1)
                    for c in range(DC):
                        mm = pe.transpose(bank[6 + t % 2][0:n, c * P:(c + 1) * P], yT[:, r, c, s0:s0 + n], ident[:, :])
                    mm.then_inc(yr_done, 1)

            def expert(e, r, first):
                pe.wait_ge(w1_in[r], (e - r) * 8 + 16)
                for j in range(HC):
                    if not (first and j < 4):
                        pe.wait_ge(h_done, e * HC + (j - 3))
                    for c in range(DC):
                        mm = pe.matmul(bank[j % 4][:, 0:CAP], w1_sb[:, r, c, j * P:(j + 1) * P],
                                       xT[:, c, bass.ds(e * CAP, CAP)], start=(c == 0), stop=(c == DC - 1))
                    mm.then_inc(l1_done, 1)
                if not first:
                    slot_rows(e - 1, 1 - r)
                pe.wait_ge(w2_in[r], (e - r) * 8 + 16)
                pe.wait_ge(h_done, (e + 1) * HC)
                for c in range(DC):
                    for j in range(HC):
                        mm = pe.matmul(bank[4 + c][:, 0:CAP], w2_sb[:, r, j, c * P:(c + 1) * P], hT[:, r, j, :],
                                       start=(j == 0), stop=(j == HC - 1))
                    mm.then_inc(l2_done, 1)

            expert_loop(pe, expert)
            slot_rows(E - 1, 1)


WACT = 5
KDVE = 6


def kernel(x, L0_tok_W, L0_tok_b, L0_attn_Wq, L0_attn_Wk, L0_attn_Wv, L0_attn_Wo, L0_attn_lambda_q1,
           L0_attn_lambda_k1, L0_attn_lambda_q2, L0_attn_lambda_k2, L0_attn_gamma, L0_attn_beta,
           L0_ffn_Wg, L0_ffn_W1, L0_ffn_b1, L0_ffn_W2, L0_ffn_b2):
    import concourse.bacc as _bacc
    from concourse.bass_utils import run_bass_kernel_spmd as _run

    def rows_first(w):
        return np.ascontiguousarray(w.reshape(w.shape[0] // P, P, w.shape[1]).transpose(1, 0, 2))

    a = SIDE // PATCH
    img = np.asarray(x).reshape(IMGS, CH, a, PATCH, a, PATCH).transpose(3, 5, 1, 0, 2, 4).reshape(IN, N)
    xh = np.ascontiguousarray(img.reshape(IC, P, G, P).transpose(1, 2, 0, 3))
    n = np.asarray
    ins = {
        "xh": xh,
        "wt": rows_first(n(L0_tok_W).T),
        "tok_b": n(L0_tok_b),
        "wq": rows_first(n(L0_attn_Wq)), "wk": rows_first(n(L0_attn_Wk)),
        "wv": rows_first(n(L0_attn_Wv)), "wo": rows_first(n(L0_attn_Wo)),
        "lam": np.stack([n(L0_attn_lambda_q1), n(L0_attn_lambda_k1), n(L0_attn_lambda_q2),
                         n(L0_attn_lambda_k2)]).reshape(2, 2, HD),
        "gamma": n(L0_attn_gamma), "beta": n(L0_attn_beta),
        "wg": rows_first(n(L0_ffn_Wg)),
        "w1": np.ascontiguousarray(n(L0_ffn_W1).reshape(E, DC, P, HID).transpose(0, 2, 1, 3)),
        "b1": np.ascontiguousarray(n(L0_ffn_b1).reshape(E, HC, P).transpose(2, 0, 1)),
        "w2": np.ascontiguousarray(n(L0_ffn_W2).reshape(E, HC, P, D).transpose(0, 2, 1, 3)),
        "b2": np.ascontiguousarray(n(L0_ffn_b2).reshape(E, DC, P).transpose(2, 0, 1)),
    }
    nc = _bacc.Bacc("TRN2", target_bir_lowering=False, num_devices=1)
    args = [nc.dram_tensor(f"in_{k}", v.shape, F32, kind="ExternalInput").ap() for k, v in ins.items()]
    out = nc.dram_tensor("out", (N, D), F32, kind="ExternalOutput").ap()
    vit_tower(nc, *args, out)
    r = _run(nc, [{f"in_{k}": v for k, v in ins.items()}], core_ids=[0])
    return r.results[0]["out"].reshape(IMGS, S, D)
```

```python
import numpy as np
import concourse.bass as bass
from concourse import mybir
from contextlib import ExitStack
import math

F32 = mybir.dt.float32
F32R = mybir.dt.float32r
U32 = mybir.dt.uint32
BF16 = mybir.dt.bfloat16
ALU = mybir.AluOpType
ACT = mybir.ActivationFunctionType
AX = mybir.AxisListType

P = 128
IMGS, CH, SIDE, PATCH = 64, 3, 64, 16
S = (SIDE // PATCH) ** 2
N = IMGS * S
G = N // P
GI = P // S
D = 256
DC = D // P
IN = PATCH * PATCH * CH
IC = IN // P
HEADS, HD = 16, 16
QC = 2 * D // P
HB = P // HD
NHB = 2 * HEADS
SCALE = HD ** -0.5
LAMBDA_INIT = 0.8 - 0.6 * math.exp(-0.3 * 11)
EPS = 1e-5
E, K, HID = 8, 2, 1024
HC = HID // P
CAP = int(math.ceil(N * K / E * 1.05))
SLOTS = E * CAP
NS = CAP + CAP % 2
SP2 = CAP // P
ST = CAP - SP2 * P
assert SP2 == 2 and 0 < ST <= 128 and DC == 2
META = 4
ROW = D + META
MADE = 17
TURNS = SP2 + 1
WQ = 4
W1C, W2C = DC * HID // WQ, HC * D // WQ
WACT = 4
KDVE = 6


def vit_tower(nc, xh, wt, tok_b, wq, wk, wv, wo, lam, gamma, beta, wg, w1, b1, w2, b2, out):
    ctx = ExitStack()
    with ctx:
        def sb(name, shape, dt=F32):
            return ctx.enter_context(nc.sbuf_tensor(name, shape, dt))

        def sem(name):
            return ctx.enter_context(nc.semaphore(name))

        xbuf = nc.dram_tensor("xbuf", (SLOTS + K * N, ROW), F32, kind="Internal").ap()

        wg_sb = sb("wg_sb", [P, DC, E])
        b1_sb = sb("b1_sb", [P, E, HC])
        b2_sb = sb("b2_sb", [P, E, DC])
        rows = sb("rows", [P, 3, D])
        ident = sb("ident", [P, P])
        same = sb("same", [P, GI, S])
        upper = sb("upper", [P, P])
        ones = sb("ones", [P, P])
        warm = sb("warm", [P, 1])
        half = sb("half", [P, 1])
        iota8 = sb("iota8", [P, E])
        trash = sb("trash", [P, G, K])
        token = sb("token", [P, G])
        empty = sb("empty", [P, TURNS, ROW])
        h_sb = sb("h_sb", [P, G, D])
        t1 = sb("t1", [P, D])
        t2 = sb("t2", [P, D])
        x2T = sb("x2T", [P, DC, P])
        xrow = sb("xrow", [P, 2, ROW])
        stat = sb("stat", [P, 2, 6])
        mv = sb("mv", [P, 2, 2])
        var = sb("var", [P, 2])
        rstd = sb("rstd", [P, 2])
        stat1 = sb("stat1", [P, 2, 6])
        mv1 = sb("mv1", [P, 2, 2])
        var1 = sb("var1", [P, 2])
        rstd1 = sb("rstd1", [P, 2])
        mx = sb("mx", [P, NHB])
        sm = sb("sm", [P, NHB])
        rc = sb("rc", [P, NHB])
        lmax = sb("lmax", [P, 8])
        ld = sb("ld", [P, E])
        le = sb("le", [P, E])
        top = sb("top", [P, 8])
        topi = sb("topi", [P, 8], U32)
        topf = sb("topf", [P, K])
        oh = sb("oh", [P, K, E])
        sel = sb("sel", [P, E])
        prev = sb("prev", [P, E])
        gs = sb("gs", [P, 2])
        junk = sb("junk", [P, K, E])
        pos = sb("pos", [P, K])
        keep = sb("keep", [P, K])
        dest = sb("dest", [P, K])
        dsc = sb("dsc", [P, K])
        send = sb("send", [P, G, K], U32)
        w1_sb = sb("w1_sb", [P, 2, DC * HID])
        w2_sb = sb("w2_sb", [P, 2, HC * D])
        xg = sb("xg", [P, 2, TURNS, ROW])

        front = ExitStack()

        def sbf(name, shape, dt=F32):
            return front.enter_context(nc.sbuf_tensor(name, shape, dt))

        x_sb = sbf("x_sb", [P, G, IC, P])
        wt_sb = sbf("wt_sb", [P, IC, D])
        xn = sbf("xn", [P, 2, D])
        kblk = sbf("kblk", [P, 3, QC * GI, HB, S], BF16)
        q3 = sbf("q3", [P, 2, 3, QC, P], BF16)
        k3 = sbf("k3", [P, 3, QC * GI, S], BF16)
        pf = sbf("pf", [P, HEADS, P])
        pw = sbf("pw", [P, HEADS, GI, S])
        wq_sb = sbf("wq_sb", [P, DC, 2 * D])
        wk_sb = sbf("wk_sb", [P, DC, 2 * D])
        wv_sb = sbf("wv_sb", [P, DC, D])
        wo_sb = sbf("wo_sb", [P, DC, D])
        xnT = sbf("xnT", [P, DC, N])
        q_rest = sbf("q_rest", [P, QC * P])
        k_rest = sbf("k_rest", [P, QC * P])
        v_sb = sbf("v_sb", [P, 2, D])
        c_sb = sbf("c_sb", [P, 2, 2, GI, S])
        bc = sbf("bc", [P, 2, 2, GI, S])
        sT = sbf("sT", [P, QC, P])
        sd = sbf("sd", [P, NHB, S])
        ex = sbf("ex", [P, NHB, S])
        prob = sbf("prob", [P, HEADS, S])
        o_sb = sbf("o_sb", [P, D])
        oT = sbf("oT", [P, DC, P])
        lam_sb = sbf("lam_sb", [P, 2, 2, HD])
        lam_pr = sbf("lam_pr", [P, 2, HD])
        lam_s = sbf("lam_s", [P, 2])
        lam_e = sbf("lam_e", [P, 2])
        neglam = sbf("neglam", [P, 2])
        front.close()

        def parts(name, cols):
            return sb(name + "_hi", [P, cols], F32R), sb(name + "_lo", [P, cols], F32R)

        w1p, w2p = [None] * 2, [None] * 2
        for r in range(2):
            w1p[r] = parts(f"w1p{r}", DC * HID)
            w2p[r] = parts(f"w2p{r}", HC * D)
        hp = [parts(f"hp{j}", NS) for j in range(HC)]
        xp = [parts(f"xp{r}", DC * NS) for r in range(2)]
        hf = sb("hf", [P, 4, NS])
        meta = sb("meta", [P, 2, TURNS, META])
        choice = sb("choice", [P, 2, TURNS])
        weigh = sb("weigh", [P, 2, TURNS])
        back = sb("back", [P, 2, TURNS], U32)
        yT = sb("yT", [P, 2, DC, CAP])
        yr = sb("yr", [P, 2, TURNS, D])

        psum = ctx.enter_context(nc.psum_tensor("psum", [P, 8, 512], F32))
        bank = [psum[:, i, :] for i in range(8)]

        s48 = psum[:, 2:4, 0:3 * P].rearrange("p q (i n s) -> p q i n s", i=GI, n=3)

        xt_whole = bank[7].rearrange("p (c s) -> p c s", c=DC)
        xt_rest = bank[3][:, 0:DC * ST].rearrange("p (c s) -> p c s", c=DC)
        y_whole = bank[6].rearrange("p (t d) -> p t d", t=SP2)
        y_rest = bank[3][0:ST, D:2 * D]

        def slot_columns(part):
            cols = part[:, :].rearrange("p (c s) -> p c s", c=DC)
            return cols[:, :, 0:SP2 * P], cols[:, :, SP2 * P:CAP]

        x_in = [sem(f"x_in{g}") for g in range(G)]
        wt_in, rows_in, lam_in, wk_in, wq_in, wv_in, wo_in, small_in = (sem(n) for n in (
            "wt_in", "rows_in", "lam_in", "wk_in", "wq_in", "wv_in", "wo_in", "small_in"))
        zeroed = sem("zeroed")
        w1_in = [sem(f"w1_in{i}") for i in range(2)]
        w2_in = [sem(f"w2_in{i}") for i in range(2)]
        xg_in = [sem(f"xg_in{i}") for i in range(2)]
        made, lam_dve, lam_exp = sem("made"), sem("lam_dve"), sem("lam_exp")
        step = sem("step")
        emb_done, h_ready, ln1_var, ln1_rstd, xn_ready, xnt_done, xnt_ready = (sem(n) for n in (
            "emb_done", "h_ready", "ln1_var", "ln1_rstd", "xn_ready", "xnt_done", "xnt_ready"))
        q_done, k_done, v_done, q_hi, k_hi, q_res, k_res, q_mid, k_mid, q_lo, k_lo, v_ready, kblk_dve, kblk_pool = (
            sem(n) for n in ("q_done", "k_done", "v_done", "q_hi", "k_hi", "q_res", "k_res", "q_mid", "k_mid",
                             "q_lo", "k_lo", "v_ready", "kblk_dve", "kblk_pool"))
        st_done, c_ready, st_ready, s_done, sd_ready, ex_ready, pn_ready, p_ready, pt_done, pf_ready, pv_done = (sem(n) for n in (
            "st_done", "c_ready", "st_ready", "s_done", "sd_ready", "ex_ready", "pn_ready", "p_ready", "pt_done", "pf_ready", "pv_done"))
        pw_act, pw_pool = sem("pw_act"), sem("pw_pool")
        o_ready, ot_done, ot_ready, wo_done, wo_read = (sem(n) for n in (
            "o_ready", "ot_done", "ot_ready", "wo_done", "wo_read"))
        lno_var, lno_rstd, ln2_var, ln2_rstd, x2_ready, x2t_done, x2t_ready, lg_done, ld_ready, le_ready = (
            sem(n) for n in ("lno_var", "lno_rstd", "ln2_var", "ln2_rstd", "x2_ready", "x2t_done",
                             "x2t_ready", "lg_done", "ld_ready", "le_ready"))
        sel_ready, cum_done, cum_read, send_ready = (sem(n) for n in (
            "sel_ready", "cum_done", "cum_read", "send_ready"))
        sent = [sem(f"sent{i}") for i in range(2)]
        w1_hi, w1_lo, w2_hi, w2_lo_pool, w2_lo_dve = (sem(n) for n in (
            "w1_hi", "w1_lo", "w2_hi", "w2_lo_pool", "w2_lo_dve"))
        meta_ready, w_half, w_ready, back_ready = (sem(n) for n in ("meta_ready", "w_half", "w_ready", "back_ready"))
        padded, xt_done, x_hi, x_lo, l1_done, h_done, h_hi, h_lo, l2_done, yt_ready, yr_done, yr_ready = (
            sem(n) for n in ("padded", "xt_done", "x_hi", "x_lo", "l1_done", "h_done", "h_hi", "h_lo", "l2_done",
                             "yt_ready", "yr_done", "yr_ready"))
        base_done, added = sem("base_done"), sem("added")

        block = ctx.enter_context(nc.Block())


        def expert_loop(eng, body):
            for e in range(2):
                body(e, e)
            with eng.Fori(1, E // 2 - 1) as i:
                for r in range(2):
                    body(i * 2 + r, r)
            for e in (E - 2, E - 1):
                body(e, e % 2)

        def first(e):
            return isinstance(e, int) and e == 0

        def last(e):
            return isinstance(e, int) and e == E - 1

        def turns(e, r):
            return e - r

        def rows_free(eng, e):
            if last(e):
                eng.wait_ge(added, 16 * TURNS * (E - 2))
            elif not (isinstance(e, int) and e < 2):
                eng.wait_ge(w2_lo_pool, (e + 1) * (WQ // 2) + 1)

        @block.sync
        def _(sp):
            sp.dma_start(x_sb[:, 0, :, :], xh[:, 0, :, :]).then_inc(x_in[0], 16)
            sp.dma_start(wt_sb[:, :, :], wt).then_inc(wt_in, 16)
            for n, r in enumerate((tok_b, gamma, beta)):
                sp.dma_start(rows[:, n, :], r.partition_broadcast(P)).then_inc(rows_in, 16)
            sp.dma_start(x_sb[:, 1, :, :], xh[:, 1, :, :]).then_inc(x_in[1], 16)
            sp.dma_start(wk_sb[:, :, :], wk).then_inc(wk_in, 16)
            sp.dma_start(lam_sb[:, :, :, :], lam.partition_broadcast(P)).then_inc(lam_in, 16)
            sp.dma_start(wq_sb[:, :, :], wq).then_inc(wq_in, 16)
            sp.dma_start(wv_sb[:, :, :], wv).then_inc(wv_in, 16)
            sp.dma_start(x_sb[:, 2, :, :], xh[:, 2, :, :]).then_inc(x_in[2], 16)
            sp.dma_start(wo_sb[:, :, :], wo).then_inc(wo_in, 16)
            for t, s in ((wg_sb, wg), (b1_sb, b1), (b2_sb, b2)):
                sp.dma_start(t[:, :, :], s).then_inc(small_in, 16)
            for g in range(3, G):
                sp.dma_start(x_sb[:, g, :, :], xh[:, g, :, :]).then_inc(x_in[g], 16)

            def slots(buf, row):
                whole = buf[bass.ds(row, SP2 * P), :].rearrange("(p t) d -> p t d", t=SP2)
                return whole, buf[bass.ds(row + SP2 * P, ST), :]

            sp.wait_ge(made, 15)
            for e in range(E):
                whole, rest_ = slots(xbuf, e * CAP)
                sp.dma_start(whole, empty[:, 0:SP2, :]).then_inc(zeroed, 16)
                sp.dma_start(rest_, empty[0:ST, SP2, :]).then_inc(zeroed, 16)
            whole, rest_ = slots(out, N)
            sp.dma_start(whole, empty[:, 0:SP2, 0:D]).then_inc(base_done, 16)
            sp.dma_start(rest_, empty[0:ST, SP2, 0:D]).then_inc(base_done, 16)
            for e in range(2):
                sp.dma_start(w1_sb[:, e, :], w1[e, :, :]).then_inc(w1_in[e], 16)
                sp.dma_start(w2_sb[:, e, :], w2[e, :, :]).then_inc(w2_in[e], 16)

            def fetch_slots(e, r):
                whole, rest_ = slots(xbuf, e * CAP)
                sp.dma_start(xg[:, r, 0:SP2, :], whole).then_inc(xg_in[r], 16)
                sp.dma_start(xg[0:ST, r, SP2, :], rest_).then_inc(xg_in[r], 16)

            for g in range(G):
                sp.wait_ge(ln2_var, g + 1)
                sp.dma_start(out[g * P:(g + 1) * P, :], h_sb[:, g, :]).then_inc(base_done, 16)
            for r in range(2):
                sp.wait_ge(sent[r], 16 * K * (G // 2))
            for r in range(2):
                fetch_slots(r, r)

            def expert(e, r):
                if not (isinstance(e, int) and e >= E - 2):
                    sp.wait_ge(w1_lo, (e + 1) * WQ)
                    sp.dma_start(w1_sb[:, r, :], w1[e + 2, :, :]).then_inc(w1_in[r], 16)
                    sp.wait_ge(w2_lo_pool, (e + 1) * (WQ // 2))
                    sp.wait_ge(w2_lo_dve, (e + 1) * (WQ // 2))
                    sp.dma_start(w2_sb[:, r, :], w2[e + 2, :, :]).then_inc(w2_in[r], 16)
                    sp.wait_ge(xt_done, (e + 1) * 2)
                    sp.wait_ge(meta_ready, e + 1)
                    fetch_slots(e + 2, r)

            expert_loop(sp, expert)
            sp.wait_ge(added, 16 * TURNS * E)

        @block.gpsimd
        def _(pool):
            pool.memset(empty[:, :, :], 0.0).then_inc(made, 1)
            pool.memset(ident[:, :], 0.0).then_inc(made, 1)
            pool.memset(same[:, :, :], 1.0).then_inc(made, 1)
            pool.memset(upper[:, :], 1.0).then_inc(made, 1)
            pool.memset(ones[:, :], 1.0).then_inc(made, 1)
            pool.memset(half[:, :], -0.5).then_inc(made, 1)
            pool.memset(prev[:, :], 0.0).then_inc(made, 1)
            pool.iota(iota8[:, :], pattern=[[1, E]], base=0, channel_multiplier=0,
                      allow_small_or_imprecise_dtypes=True).then_inc(made, 1)
            pool.iota(trash[:, :, :], pattern=[[K * P, G], [P, K]], base=SLOTS, channel_multiplier=1,
                      allow_small_or_imprecise_dtypes=True).then_inc(made, 1)
            pool.iota(token[:, :], pattern=[[P, G]], base=0, channel_multiplier=1,
                      allow_small_or_imprecise_dtypes=True).then_inc(made, 1)
            pool.memset(xg[:, :, SP2, D:ROW], 0.0).then_inc(made, 1)
            pool.wait_ge(made, 11)
            pool.iota(empty[:, 0:SP2, D], pattern=[[1, SP2]], base=N, channel_multiplier=SP2,
                      allow_small_or_imprecise_dtypes=True).then_inc(made, 1)
            pool.iota(empty[:, SP2, D:D + 1], pattern=[[1, 1]], base=N + SP2 * P, channel_multiplier=1,
                      allow_small_or_imprecise_dtypes=True).then_inc(made, 1)
            pool.affine_select(out=ident[:, :], in_=ident[:, :], compare_op=ALU.not_equal, fill=1.0, base=0,
                               pattern=[[-1, P]], channel_multiplier=1).then_inc(made, 1)
            pool.affine_select(out=same[:, :, :], in_=same[:, :, :], compare_op=ALU.is_ge, fill=0.0, base=0,
                               pattern=[[-S, GI], [0, S]], channel_multiplier=1).then_inc(made, 1)
            pool.wait_ge(made, 15)
            pool.affine_select(out=same[:, :, :], in_=same[:, :, :], compare_op=ALU.is_ge, fill=0.0, base=S - 1,
                               pattern=[[S, GI], [0, S]], channel_multiplier=-1).then_inc(made, 1)
            pool.affine_select(out=upper[:, :], in_=upper[:, :], compare_op=ALU.is_gt, fill=0.0, base=0,
                               pattern=[[1, P]], channel_multiplier=-1).then_inc(made, 1)
            pool.wait_ge(made, MADE)

            def power(var_sem, rstd_sem, src, dst, g):
                pool.wait_ge(var_sem, g + 1)
                pool.tensor_tensor(dst, src, half[:, :], ALU.pow).then_inc(rstd_sem, 1)

            def embed_power(g):
                power(ln1_var, ln1_rstd, var1[:, g % 2:g % 2 + 1], rstd1[:, g % 2:g % 2 + 1], g)

            embed_power(0)

            def tick(t):
                a, b, c, d = t, t - 1, t - 2, t - 3
                if d >= 0:
                    power(lno_var, lno_rstd, var[:, 0:1], rstd[:, 0:1], d)
                if a + 1 < G:
                    embed_power(a + 1)
                if d >= 1:
                    send_rows(d - 1)
                if a < G:
                    pool.wait_ge(k_mid, a + 1)
                    pool.tensor_tensor(k3[:, 2, :, :], k_rest[:, :], k3[:, 1, :, :], ALU.subtract).then_inc(k_lo, 1)
                if d >= 0:
                    power(ln2_var, ln2_rstd, var[:, 1:2], rstd[:, 1:2], d)
                if a < G:
                    pool.wait_ge(k_lo, a + 1)
                    if b >= 0:
                        pool.wait_ge(st_done, 2 * b + 2)
                    for j in range(KDVE, HB):
                        ins = pool.tensor_scalar(kblk[:, :, :, j, :], k3[:, :, :, :], same[:, j, 0:1], 1.0,
                                                 ALU.mult, ALU.mult)
                    ins.then_inc(kblk_pool, 1)
                    pool.wait_ge(q_mid, a + 1)
                    pool.tensor_tensor(q3[:, a % 2, 2, :, :], q_rest[:, :], q3[:, a % 2, 1, :, :],
                                       ALU.subtract).then_inc(q_lo, 1)
                if 0 <= b < G:
                    pool.wait_ge(pn_ready, b + 1)
                    if b >= 1:
                        pool.wait_ge(pw_act, b)
                        pool.wait_ge(pw_pool, b)
                    pair = ex[:, :, :].rearrange("p (h b) s -> p h b s", b=2)
                    pool.tensor_tensor(prob[:, :, :], pair[:, :, 0, :], pair[:, :, 1, :], ALU.add).then_inc(p_ready, 1)
                    pool.wait_ge(p_ready, b + 1)
                    if b >= 1:
                        pool.wait_ge(pt_done, 4 * b)
                    for i in range(WACT, GI):
                        ins = pool.tensor_scalar(pw[:, :, i, :], prob[:, :, :], same[:, i, 0:1], 1.0, ALU.mult, ALU.mult)
                    ins.then_inc(pw_pool, 1)
            def send_rows(g):
                if g == 0:
                    pool.wait_ge(zeroed, 16 * 2 * E)
                pool.wait_ge(send_ready, g + 1)
                for k in range(K):
                    pool.indirect_dma_start(
                        out=xbuf[:, :], out_offset=bass.IndirectOffsetOnAxis(ap=send[:, g, k:k + 1], axis=0),
                        in_=xrow[:, g % 2, :], in_offset=None).then_inc(sent[g % 2], 16)

            for t in range(G + 3):
                tick(t)

            def split_first(e, r):
                for q in range(WQ):
                    pool.wait_ge(w1_hi, e * WQ + q + 1)
                    c = slice(q * W1C, (q + 1) * W1C)
                    pool.tensor_tensor(w1p[r][1][:, c], w1_sb[:, r, c], w1p[r][0][:, c], ALU.subtract).then_inc(w1_lo, 1)

            def split_second(e, r, q):
                pool.wait_ge(w2_hi, e * WQ + q + 1)
                c = slice(q * W2C, (q + 1) * W2C)
                pool.tensor_tensor(w2p[r][1][:, c], w2_sb[:, r, c], w2p[r][0][:, c], ALU.subtract).then_inc(w2_lo_pool, 1)

            def expert(e, r):
                if not last(e):
                    split_first(e + 1, 1 - r)
                if not first(e):
                    pool.wait_ge(yr_ready, e * 2)
                    pool.wait_ge(back_ready, e)
                    if isinstance(e, int) and e == 1:
                        pool.wait_ge(base_done, 16 * (G + 2))
                    else:
                        pool.wait_ge(added, (e - 1) * (16 * TURNS))
                if not last(e):
                    split_second(e + 1, 1 - r, 0)
                if not first(e):
                    add_rows(e - 1, 1 - r)
                if not last(e):
                    split_second(e + 1, 1 - r, 1)

            def add_rows(e, r):
                for t in range(TURNS):
                    n = P if t < SP2 else ST
                    pool.indirect_dma_start(
                        out=out[:, :], out_offset=bass.IndirectOffsetOnAxis(ap=back[0:n, r, t:t + 1], axis=0),
                        in_=yr[0:n, r, t, :], in_offset=None, compute_op=ALU.add).then_inc(added, 16)

            send_rows(G - 1)
            split_first(0, 0)
            for q in range(WQ // 2):
                split_second(0, 0, q)
            expert_loop(pool, expert)
            pool.wait_ge(yr_ready, E * 2)
            pool.wait_ge(back_ready, E)
            pool.wait_ge(added, (E - 1) * (16 * TURNS))
            add_rows(E - 1, 1)

        @block.scalar
        def _(act):
            def columns_out(g):
                act.wait_ge(xnt_done, g + 1)
                act.activation(xnT[:, :, g * P:(g + 1) * P], bank[0][:, 0:D].rearrange("p (c t) -> p c t", c=DC),
                               ACT.Copy).then_inc(xnt_ready, 1)

            columns_out(0)
            act.wait_ge(lam_dve, 1)
            act.activation(lam_e[:, :], lam_s[:, :], ACT.Exp).then_inc(lam_exp, 1)

            def third(b, h):
                act.wait_ge(st_done, 2 * b + h + 1)
                if b >= 1:
                    act.wait_ge(st_ready, 2 * b + h - 1)
                act.activation(c_sb[:, h, :, :, :], s48[:, :, :, 2, :], ACT.Copy).then_inc(c_ready, 1)

            def key_high(g):
                act.wait_ge(k_done, g + 1)
                if g >= 1:
                    act.wait_ge(kblk_dve, g)
                    act.wait_ge(kblk_pool, g)
                act.activation(k3[:, 0, :, :], bank[0][:, :], ACT.Copy).then_inc(k_hi, 1)

            def prob_out(c, n):
                act.wait_ge(pt_done, 4 * c + n + 1)
                if n == 0 and c >= 1:
                    act.wait_ge(pv_done, c)
                act.activation(pf[:, 4 * n:4 * n + 4, :], bank[4 + n % 2][:, :], ACT.Copy).then_inc(pf_ready, 1)

            def tick(t):
                a, b, c, d = t, t - 1, t - 2, t - 3
                if 0 <= b < G:
                    third(b, 1)
                if 0 <= c < G:
                    prob_out(c, 0)
                    prob_out(c, 1)
                if a < G:
                    act.wait_ge(k_res, a + 1)
                    act.activation(k3[:, 1, :, :], k_rest[:, :], ACT.Copy).then_inc(k_mid, 1)
                if 0 <= c < G:
                    prob_out(c, 2)
                    prob_out(c, 3)
                if a + 1 < G:
                    columns_out(a + 1)
                if a < G:
                    act.wait_ge(q_done, a + 1)
                    if a >= 2:
                        act.wait_ge(st_done, 2 * (a - 1))
                    act.activation(q3[:, a % 2, 0, :, :], bank[1][:, :], ACT.Copy).then_inc(q_hi, 1)
                if d >= 0:
                    act.wait_ge(x2t_done, d + 1)
                    act.activation(x2T[:, :, :], bank[7][:, 0:D], ACT.Copy).then_inc(x2t_ready, 1)
                if a < G:
                    act.wait_ge(q_res, a + 1)
                    act.activation(q3[:, a % 2, 1, :, :], q_rest[:, :], ACT.Copy).then_inc(q_mid, 1)
                if 0 <= b < G:
                    act.wait_ge(sd_ready, b + 1)
                    act.activation(ex[:, :, :], sd[:, :, :], ACT.Exp, scale=SCALE).then_inc(ex_ready, 1)
                if a < G:
                    act.wait_ge(v_done, a + 1)
                    if a >= 2:
                        act.wait_ge(pv_done, a - 1)
                    act.activation(v_sb[:, a % 2, :], bank[4][:, 0:D], ACT.Copy).then_inc(v_ready, 1)
                if 0 <= c < G:
                    act.wait_ge(pv_done, c + 1)
                    act.activation(o_sb[:, :], bank[6][:, 0:D], ACT.Copy).then_inc(o_ready, 1)
                if d >= 0:
                    act.wait_ge(ld_ready, d + 1)
                    act.activation(le[:, :], ld[:, :], ACT.Exp).then_inc(le_ready, 1)
                if 0 <= c < G:
                    act.wait_ge(ot_done, c + 1)
                    act.activation(oT[:, :, :], bank[6][:, D:2 * D], ACT.Copy).then_inc(ot_ready, 1)
                if a < G:
                    third(a, 0)
                if 0 <= b < G:
                    act.wait_ge(p_ready, b + 1)
                    if b >= 1:
                        act.wait_ge(pt_done, 4 * b)
                    for i in range(WACT):
                        ins = act.activation(pw[:, :, i, :], prob[:, :, :], ACT.Copy, scale=same[:, i, 0:1])
                    ins.then_inc(pw_act, 1)
                if a + 1 < G:
                    key_high(a + 1)

            key_high(0)
            for t in range(G + 3):
                tick(t)

            def expert(e, r):
                for j in range(HC):
                    act.wait_ge(l1_done, e * HC + j + 1)
                    if not (first(e) and j < 4):
                        act.wait_ge(h_lo, e * HC + (j - 3))
                    act.activation(hf[:, j % 4, :], bank[j % 3][:, 0:NS], ACT.Gelu_apprx_tanh,
                                   bias=b1_sb[:, bass.ds(e, 1), j]).then_inc(h_done, 1)
                    if not last(e) and j % 2 == 1:
                        w1_high(e + 1, 1 - r, j // 2)
                if not first(e):
                    rows_out(e - 1, 1 - r)
                if not last(e):
                    slots_high(e + 1, 1 - r)
                    for q in range(WQ):
                        w2_high(e + 1, 1 - r, q)

            def w1_high(e, r, q):
                if q == 0:
                    act.wait_ge(w1_in[r], turns(e, r) * 8 + 16)
                c = slice(q * W1C, (q + 1) * W1C)
                act.activation(w1p[r][0][:, c], w1_sb[:, r, c], ACT.Copy).then_inc(w1_hi, 1)

            def w2_high(e, r, q):
                if q == 0:
                    act.wait_ge(w2_in[r], turns(e, r) * 8 + 16)
                c = slice(q * W2C, (q + 1) * W2C)
                act.activation(w2p[r][0][:, c], w2_sb[:, r, c], ACT.Copy).then_inc(w2_hi, 1)

            def slots_high(e, r):
                whole, rest_ = slot_columns(xp[r][0])
                act.wait_ge(xt_done, (e + 1) * 2)
                act.activation(whole, xt_whole, ACT.Copy)
                act.activation(rest_, xt_rest, ACT.Copy).then_inc(x_hi, 1)

            def rows_out(e, r):
                act.wait_ge(w_ready, e + 1)
                rows_free(act, e)
                act.wait_ge(yr_done, e * 2 + 1)
                act.activation(yr[0:ST, r, SP2, :], y_rest, ACT.Copy, scale=weigh[0:ST, r, SP2:TURNS]).then_inc(yr_ready, 1)
                act.wait_ge(yr_done, e * 2 + 2)
                for t in range(SP2):
                    ins = act.activation(yr[:, r, t, :], y_whole[:, t, :], ACT.Copy, scale=weigh[:, r, t:t + 1])
                ins.then_inc(yr_ready, 1)

            act.wait_ge(small_in, 48)
            act.activation(warm[:, :], half[:, :], ACT.Gelu_apprx_tanh)
            for q in range(WQ):
                w1_high(0, 0, q)
            for q in range(WQ):
                w2_high(0, 0, q)
            slots_high(0, 0)
            expert_loop(act, expert)
            rows_out(E - 1, 1)

        @block.vector
        def _(dve):
            steps = [0]

            def then(ins):
                settled(did(ins))

            def did(ins):
                steps[0] += 1
                ins.then_inc(step, 1)
                return steps[0]

            def settled(n):
                dve.wait_ge(step, n)

            dve.wait_ge(rows_in, 48)

            def embed_open(g):
                r = g % 2
                dve.wait_ge(emb_done, g + 1)
                dve.tensor_tensor(h_sb[:, g, :], bank[min(g, 1)][:, 0:D], rows[:, 0, :], ALU.add).then_inc(h_ready, 1)
                dve.wait_ge(h_ready, g + 1)
                then(dve.bn_stats(stat1[:, r, :], h_sb[:, g, :]))
                then(dve.bn_aggr(mv1[:, r, :], stat1[:, r, :]))
                dve.tensor_scalar(var1[:, r:r + 1], mv1[:, r, 1:2], EPS, None, ALU.add).then_inc(ln1_var, 1)

            def embed_close(g):
                r = g % 2
                dve.wait_ge(ln1_rstd, g + 1)
                if g >= 2:
                    dve.wait_ge(xnt_done, g - 1)
                dve.tensor_scalar(xn[:, r, :], h_sb[:, g, :], mv1[:, r, 0:1], rstd1[:, r:r + 1],
                                  ALU.subtract, ALU.mult).then_inc(xn_ready, 1)
                then(dve.tensor_tensor(h_sb[:, g, :], h_sb[:, g, :], rows[:, 2, :], ALU.add))

            embed_open(0)
            embed_close(0)
            dve.wait_ge(lam_in, 16)
            then(dve.tensor_tensor(lam_pr[:, :, :], lam_sb[:, :, 0, :], lam_sb[:, :, 1, :], ALU.mult))
            dve.reduce_sum(lam_s[:, :], lam_pr[:, :, :], AX.X).then_inc(lam_dve, 1)
            dve.wait_ge(lam_exp, 1)
            then(dve.tensor_tensor(neglam[:, 0:1], lam_e[:, 1:2], lam_e[:, 0:1], ALU.subtract))
            then(dve.tensor_scalar(neglam[:, 1:2], neglam[:, 0:1], -LAMBDA_INIT, None, ALU.add))
            dve.wait_ge(made, MADE)

            def rest(g, b, hi, first, res, lo, out):
                dve.wait_ge(hi, g + 1)
                if g >= 1:
                    dve.wait_ge(lo, g)
                dve.tensor_tensor(out[:, :], bank[b][:, :], first, ALU.subtract).then_inc(res, 1)

            def add_scores(g, h):
                dve.wait_ge(c_ready, 2 * g + h + 1)
                return did(dve.tensor_tensor(bc[:, h, :, :, :], s48[:, :, :, 1, :], c_sb[:, h, :, :, :], ALU.add))

            def add_scores_close(g, h, added_up):
                settled(added_up)
                if g >= 1:
                    dve.wait_ge(s_done, g)
                dve.tensor_tensor(sT[:, 2 * h:2 * h + 2, :].rearrange("p q (i s) -> p q i s", i=GI), s48[:, :, :, 0, :],
                                  bc[:, h, :, :, :], ALU.add).then_inc(st_ready, 1)

            def spread(g, j):
                if g >= G:
                    return
                if j == 0:
                    dve.wait_ge(k_lo, g + 1)
                    if g >= 1:
                        dve.wait_ge(st_done, 2 * g)
                ins = dve.tensor_scalar(kblk[:, :, :, j, :], k3[:, :, :, :], same[:, j, 0:1], None, ALU.mult)
                if j == KDVE - 1:
                    ins.then_inc(kblk_dve, 1)

            def norms_open(g, a):
                on = g >= 0
                if on:
                    dve.wait_ge(wo_done, g + 1)
                    n = did(dve.bn_stats(stat[:, 0, :], bank[6][:, 0:D]))
                if a < G:
                    rest(a, 0, k_hi, k3[:, 0, :, :].rearrange("p a s -> p (a s)"), k_res, k_lo, k_rest)
                if on:
                    settled(n)
                    then(dve.bn_aggr(mv[:, 0, :], stat[:, 0, :]))
                    dve.tensor_scalar(var[:, 0:1], mv[:, 0, 1:2], EPS, None, ALU.add).then_inc(lno_var, 1)

            def norms_middle(g):
                dve.wait_ge(lno_rstd, g + 1)
                dve.tensor_scalar(t1[:, :], bank[6][:, 0:D], mv[:, 0, 0:1], rstd[:, 0:1],
                                  ALU.subtract, ALU.mult).then_inc(wo_read, 1)
                dve.wait_ge(wo_read, g + 1)
                then(dve.tensor_tensor(t2[:, :], t1[:, :], rows[:, 1, :], ALU.mult))
                then(dve.tensor_tensor(h_sb[:, g, :], t2[:, :], h_sb[:, g, :], ALU.add))
                then(dve.bn_stats(stat[:, 1, :], h_sb[:, g, :]))
                then(dve.bn_aggr(mv[:, 1, :], stat[:, 1, :]))
                dve.tensor_scalar(var[:, 1:2], mv[:, 1, 1:2], EPS, None, ALU.add).then_inc(ln2_var, 1)

            def norms_close(g):
                dve.wait_ge(ln2_rstd, g + 1)
                if g >= 2:
                    dve.wait_ge(sent[g % 2], 16 * K * (g // 2))
                dve.tensor_scalar(xrow[:, g % 2, 0:D], h_sb[:, g, :], mv[:, 1, 0:1], rstd[:, 1:2],
                                  ALU.subtract, ALU.mult).then_inc(x2_ready, 1)
                dve.tensor_copy(xrow[:, g % 2, D:D + 1], token[:, g:g + 1])

            def route_open(g):
                dve.wait_ge(lg_done, g + 1)
                then(dve.max(lmax[:, :], bank[7][:, D:D + E]))
                dve.tensor_scalar(ld[:, :], bank[7][:, D:D + E], lmax[:, 0:1], None, ALU.subtract).then_inc(ld_ready, 1)

            def route_middle(g):
                dve.wait_ge(le_ready, g + 1)
                n = did(dve.max(top[:, :], le[:, :]))
                settled(n)
                n = did(dve.max_index(topi[:, :], top[:, :], le[:, :]))
                settled(n)
                n = did(dve.tensor_copy(topf[:, :], topi[:, 0:K]))
                settled(n)
                dve.tensor_scalar(oh[:, 0, :], iota8[:, :], topf[:, 0:1], None, ALU.is_equal)
                n = did(dve.tensor_scalar(oh[:, 1, :], iota8[:, :], topf[:, 1:2], None, ALU.is_equal))
                m = did(dve.tensor_tensor(gs[:, 0:1], top[:, 0:1], top[:, 1:2], ALU.add))
                if g >= 1:
                    dve.wait_ge(cum_done, g)
                    settled(m)
                    n = did(dve.tensor_tensor(prev[:, :], prev[:, :], sel[:, :], ALU.add))
                settled(m)
                m = did(dve.reciprocal(gs[:, 1:2], gs[:, 0:1]))
                settled(n)
                dve.tensor_tensor(sel[:, :], oh[:, 0, :], oh[:, 1, :], ALU.add).then_inc(sel_ready, 1)
                settled(m)
                dve.tensor_scalar(xrow[:, g % 2, D + 2:ROW], top[:, 0:K], gs[:, 1:2], None, ALU.mult)
                dve.tensor_copy(xrow[:, g % 2, D + 1:D + 2], topf[:, 0:1])

            def softmax_open(g):
                s3 = bank[2][:, :].rearrange("p (a s) -> p a s", s=S)
                dve.wait_ge(s_done, g + 1)
                then(dve.reduce_max(mx[:, :], s3, AX.X))
                dve.tensor_tensor(sd[:, :, :], s3, mx[:, :].unsqueeze(2).broadcast_to([P, NHB, S]),
                                  ALU.subtract).then_inc(sd_ready, 1)

            def softmax_close(g, a):
                dve.wait_ge(ex_ready, g + 1)
                n = did(dve.reduce_sum(sm[:, :], ex[:, :, :], AX.X))
                spread(a, KDVE - 3)
                settled(n)
                n = did(dve.reciprocal(rc[:, :], sm[:, :]))
                spread(a, KDVE - 2)
                settled(n)
                second = rc[:, :].rearrange("p (h b) -> p h b", b=2)[:, :, 1]
                n = did(dve.tensor_scalar(second, second, neglam[:, 1:2], None, ALU.mult))
                spread(a, KDVE - 1)
                settled(n)
                dve.tensor_tensor(ex[:, :, :], ex[:, :, :], rc[:, :].unsqueeze(2).broadcast_to([P, NHB, S]),
                                  ALU.mult).then_inc(pn_ready, 1)

            def route_close(g):
                dve.wait_ge(cum_done, g + 1)
                cum = bank[7][:, D + E:D + 2 * E].unsqueeze(1).broadcast_to([P, K, E])
                dve.tensor_tensor(junk[:, :, :], oh[:, :, :], cum, ALU.mult).then_inc(cum_read, 1)
                dve.wait_ge(cum_read, g + 1)
                then(dve.reduce_sum(pos[:, :], junk[:, :, :], AX.X))
                dve.tensor_scalar(keep[:, :], pos[:, :], float(CAP), None, ALU.is_lt)
                then(dve.scalar_tensor_tensor(out=dest[:, :], in0=topf[:, :], scalar=float(CAP), in1=pos[:, :],
                                              op0=ALU.mult, op1=ALU.add))
                then(dve.tensor_tensor(dsc[:, :], dest[:, :], trash[:, g, :], ALU.subtract))
                then(dve.tensor_tensor(dsc[:, :], dsc[:, :], keep[:, :], ALU.mult))
                dve.tensor_tensor(send[:, g, :], dsc[:, :], trash[:, g, :], ALU.add).then_inc(send_ready, 1)

            def tick(t):
                a, b, d = t, t - 1, t - 3
                norms_open(d, a)
                if a + 1 < G:
                    embed_open(a + 1)
                if 0 <= b < G:
                    add_scores_close(b, 1, add_scores(b, 1))
                if a + 1 < G:
                    embed_close(a + 1)
                if d >= 0:
                    norms_middle(d)
                if 0 <= b < G:
                    softmax_open(b)
                if d >= 0:
                    norms_close(d)
                if a < G:
                    rest(a, 1, q_hi, q3[:, a % 2, 0, :, :].rearrange("p q t -> p (q t)"), q_res, q_lo, q_rest)
                for j in range(KDVE - 3):
                    spread(a, j)
                if 0 <= b < G:
                    softmax_close(b, a)
                else:
                    for j in range(KDVE - 3, KDVE):
                        spread(a, j)
                if d >= 0:
                    route_open(d)
                if d >= 0:
                    route_middle(d)
                if a < G:
                    add_scores_close(a, 0, add_scores(a, 0))
                if d >= 0:
                    route_close(d)

            for t in range(G + 3):
                tick(t)

            def split_weights(e, r):
                for q in range(WQ // 2, WQ):
                    dve.wait_ge(w2_hi, e * WQ + q + 1)
                    c = slice(q * W2C, (q + 1) * W2C)
                    dve.tensor_tensor(w2p[r][1][:, c], w2_sb[:, r, c], w2p[r][0][:, c], ALU.subtract).then_inc(w2_lo_dve, 1)

            def split_slots(e, r):
                hi_whole, hi_rest = slot_columns(xp[r][0])
                lo_whole, lo_rest = slot_columns(xp[r][1])
                dve.wait_ge(x_hi, e + 1)
                dve.tensor_tensor(lo_whole, xt_whole, hi_whole, ALU.subtract)
                dve.tensor_tensor(lo_rest, xt_rest, hi_rest, ALU.subtract).then_inc(x_lo, 1)

            def high(e, j):
                dve.wait_ge(h_done, e * HC + j + 1)
                if j == 0 and not first(e):
                    dve.wait_ge(l2_done, e * DC)
                dve.tensor_copy(hp[j][0][:, :], hf[:, j % 4, :]).then_inc(h_hi, 1)

            def low(e, j):
                dve.wait_ge(h_hi, e * HC + j + 1)
                dve.tensor_tensor(hp[j][1][:, :], hf[:, j % 4, :], hp[j][0][:, :], ALU.subtract).then_inc(h_lo, 1)

            def bias_out(e, r):
                for c in range(DC):
                    dve.wait_ge(l2_done, e * DC + c + 1)
                    dve.tensor_scalar(yT[:, r, c, :], bank[4 + c][:, 0:CAP], b2_sb[:, bass.ds(e, 1), c], None,
                                      ALU.add).then_inc(yt_ready, 1)

            def weights_of_slots(e, r):
                first_one, g0, g1 = (meta[:, r, :, i] for i in range(1, META))
                dve.wait_ge(xg_in[r], turns(e, r) * 16 + 32)
                if not (isinstance(e, int) and e < 2):
                    dve.wait_ge(back_ready, e - 1)
                dve.tensor_copy(meta[:, r, :, :], xg[:, r, :, D:ROW]).then_inc(meta_ready, 1)
                dve.wait_ge(meta_ready, e + 1)
                expert_is = iota8[:, bass.ds(e, 1)]
                dve.scalar_tensor_tensor(out=choice[:, 0, :], in0=first_one, scalar=expert_is, in1=g0,
                                         op0=ALU.is_equal, op1=ALU.mult)
                dve.scalar_tensor_tensor(out=choice[:, 1, :], in0=first_one, scalar=expert_is, in1=g1,
                                         op0=ALU.not_equal, op1=ALU.mult).then_inc(w_half, 1)
                dve.wait_ge(w_half, e + 1)
                if not (isinstance(e, int) and e < 2):
                    dve.wait_ge(yr_ready, (e - 1) * 2)
                dve.tensor_tensor(weigh[:, r, :], choice[:, 0, :], choice[:, 1, :], ALU.add).then_inc(w_ready, 1)

            def tokens_of_slots(e, r):
                dve.wait_ge(meta_ready, e + 1)
                rows_free(dve, e)
                dve.tensor_copy(back[:, r, :], meta[:, r, :, 0]).then_inc(back_ready, 1)

            def expert(e, r):
                for j in range(HC):
                    high(e, j)
                    if j >= 1:
                        low(e, j - 1)
                low(e, HC - 1)
                if not first(e):
                    tokens_of_slots(e - 1, 1 - r)
                if not last(e):
                    split_slots(e + 1, 1 - r)
                    weights_of_slots(e + 1, 1 - r)
                    split_weights(e + 1, 1 - r)
                bias_out(e, r)

            for r in range(2):
                for p in xp[r]:
                    ins = dve.memset(p[:, :].bitcast(F32).rearrange("p (c s) -> p c s", c=DC)[:, :, CAP:NS], 0.0)
            ins.then_inc(padded, 1)
            split_weights(0, 0)
            split_slots(0, 0)
            weights_of_slots(0, 0)
            dve.wait_ge(small_in, 48)
            expert_loop(dve, expert)
            tokens_of_slots(E - 1, 1)

        @block.tensor
        def _(pe):
            pe.wait_ge(wt_in, 16)
            pe.wait_ge(made, MADE)

            def embed(g):
                pe.wait_ge(x_in[g], 16)
                if g >= 2:
                    pe.wait_ge(q_res, g - 1)
                for c in range(IC):
                    mm = pe.matmul(bank[min(g, 1)][:, 0:D], x_sb[:, g, c, :], wt_sb[:, c, :], start=(c == 0), stop=(c == IC - 1))
                mm.then_inc(emb_done, 1)

            def norm_transpose(g):
                pe.wait_ge(xn_ready, g + 1)
                if g >= 1:
                    pe.wait_ge(k_res, g)
                for c in range(DC):
                    mm = pe.transpose(bank[0][:, c * P:(c + 1) * P], xn[:, g % 2, c * P:(c + 1) * P], ident[:, :])
                mm.then_inc(xnt_done, 1)

            def project(g, w, b, done, read):
                pe.wait_ge(xnt_ready, g + 1)
                if g >= 1:
                    pe.wait_ge(read, g)
                if b == 1:
                    pe.wait_ge(h_ready, min(g + 2, G))
                for q in range(QC):
                    for c in range(DC):
                        mm = pe.matmul(bank[b][:, q * P:(q + 1) * P], w[:, c, q * P:(q + 1) * P],
                                       xnT[:, c, g * P:(g + 1) * P], start=(c == 0), stop=(c == DC - 1))
                mm.then_inc(done, 1)

            def project_v(g):
                if g >= 2:
                    pe.wait_ge(pf_ready, 4 * (g - 2) + 3)
                for c in range(DC):
                    mm = pe.matmul(bank[4][:, 0:D], xnT[:, c, g * P:(g + 1) * P], wv_sb[:, c, :],
                                   start=(c == 0), stop=(c == DC - 1))
                mm.then_inc(v_done, 1)

            def scores(g, h):
                if h == 0:
                    pe.wait_ge(kblk_dve, g + 1)
                    pe.wait_ge(kblk_pool, g + 1)
                    pe.wait_ge(q_lo, g + 1)
                    if g >= 1:
                        pe.wait_ge(sd_ready, g)
                else:
                    pe.wait_ge(st_ready, 2 * g + 1)
                for q in range(2):
                    for i in range(GI):
                        for n in range(3):
                            mm = pe.matmul(s48[:, q, i, n:3, :], kblk[:, n, (2 * h + q) * GI + i, :, :],
                                           q3[:, g % 2, 0:3 - n, 2 * h + q, i * S:(i + 1) * S],
                                           start=(n == 0), stop=(n == 2))
                mm.then_inc(st_done, 1)

            def score_rows(g):
                pe.wait_ge(st_ready, 2 * g + 2)
                for q in range(QC):
                    mm = pe.transpose(bank[2][:, q * P:(q + 1) * P], sT[:, q, :], ident[:, :])
                mm.then_inc(s_done, 1)

            def prob_columns(g, n):
                if n == 0:
                    pe.wait_ge(pw_act, g + 1)
                    pe.wait_ge(pw_pool, g + 1)
                    pe.wait_ge(v_ready, min(g + 2, G))
                m = 4 * g + n
                if m >= 2:
                    pe.wait_ge(pf_ready, m - 1)
                for h in range(4):
                    mm = pe.transpose(bank[4 + n % 2][:, h * P:(h + 1) * P], pw[:, 4 * n + h, :, :], ident[:, :])
                mm.then_inc(pt_done, 1)

            def weigh_values(g, half):
                if half == 0:
                    pe.wait_ge(pf_ready, 4 * g + 4)
                    pe.wait_ge(v_ready, g + 1)
                    if g >= 1:
                        pe.wait_ge(wo_read, g)
                for h in range(half * HEADS // 2, (half + 1) * HEADS // 2):
                    mm = pe.matmul(bank[6][:, h * HD:(h + 1) * HD], pf[:, h, :], v_sb[:, g % 2, h * HD:(h + 1) * HD],
                                   start=True, stop=True)
                if half == 1:
                    mm.then_inc(pv_done, 1)

            def out_project(g):
                pe.wait_ge(o_ready, g + 1)
                for c in range(DC):
                    mm = pe.transpose(bank[6][:, D + c * P:D + (c + 1) * P], o_sb[:, c * P:(c + 1) * P], ident[:, :])
                mm.then_inc(ot_done, 1)

            def out_project_close(g):
                pe.wait_ge(ot_ready, g + 1)
                for c in range(DC):
                    mm = pe.matmul(bank[6][:, 0:D], oT[:, c, :], wo_sb[:, c, :], start=(c == 0), stop=(c == DC - 1))
                mm.then_inc(wo_done, 1)

            def gate_logits(g):
                pe.wait_ge(x2_ready, g + 1)
                if g >= 1:
                    pe.wait_ge(cum_read, g)
                for c in range(DC):
                    mm = pe.transpose(bank[7][:, c * P:(c + 1) * P], xrow[:, g % 2, c * P:(c + 1) * P], ident[:, :])
                mm.then_inc(x2t_done, 1)

            def gate_logits_close(g):
                pe.wait_ge(x2t_ready, g + 1)
                for c in range(DC):
                    mm = pe.matmul(bank[7][:, D:D + E], x2T[:, c, :], wg_sb[:, c, :], start=(c == 0), stop=(c == DC - 1))
                mm.then_inc(lg_done, 1)

            def count(g):
                pe.wait_ge(sel_ready, g + 1)
                pe.matmul(bank[7][:, D + E:D + 2 * E], upper[:, :], sel[:, :], start=True, stop=False)
                pe.matmul(bank[7][:, D + E:D + 2 * E], ones[:, :], prev[:, :], start=False, stop=True).then_inc(cum_done, 1)

            def tick(t):
                a, b, c, d = t, t - 1, t - 2, t - 3
                if 0 <= b < G:
                    scores(b, 1)
                if 0 <= c < G:
                    for n in range(4):
                        prob_columns(c, n)
                if a + 1 < G:
                    norm_transpose(a + 1)
                if 0 <= b < G:
                    score_rows(b)
                if a < G:
                    project(a, wq_sb, 1, q_done, q_res)
                if 0 <= c < G:
                    weigh_values(c, 0)
                if d >= 0:
                    gate_logits(d)
                if a < G:
                    project_v(a)
                if a + 2 < G:
                    embed(a + 2)
                if d >= 0:
                    gate_logits_close(d)
                if 0 <= c < G:
                    weigh_values(c, 1)
                if a < G:
                    scores(a, 0)
                if 0 <= c < G:
                    out_project(c)
                if a + 1 < G:
                    project(a + 1, wk_sb, 0, k_done, k_res)
                if d >= 0:
                    count(d)
                if 0 <= c < G:
                    out_project_close(c)

            embed(0)
            embed(1)
            norm_transpose(0)
            for s in (wk_in, wq_in, wv_in, wo_in):
                pe.wait_ge(s, 16)
            pe.wait_ge(small_in, 48)
            project(0, wk_sb, 0, k_done, k_res)
            for t in range(G + 3):
                tick(t)

            def slots_across(e, r):
                pe.wait_ge(xg_in[r], turns(e, r) * 16 + 32)
                if not first(e):
                    pe.wait_ge(x_lo, e)
                for c in range(DC):
                    if c == 1 and not (isinstance(e, int) and e < 2):
                        pe.wait_ge(yr_ready, (e - 2) * 2 + 1)
                    for t in range(SP2):
                        mm = pe.transpose(xt_whole[:, c, t * P:(t + 1) * P], xg[:, r, t, c * P:(c + 1) * P], ident[:, :])
                mm.then_inc(xt_done, 1)
                for c in range(DC):
                    mm = pe.transpose(xt_rest[:, c, :], xg[0:ST, r, SP2, c * P:(c + 1) * P], ident[0:ST, 0:ST])
                mm.then_inc(xt_done, 1)

            def slot_rows(e, r):
                pe.wait_ge(yt_ready, (e + 1) * DC)
                if not first(e):
                    pe.wait_ge(yr_ready, e * 2)
                for c in range(DC):
                    mm = pe.transpose(y_rest[:, c * P:(c + 1) * P], yT[:, r, c, SP2 * P:CAP], ident[:, :])
                mm.then_inc(yr_done, 1)
                for c in range(DC):
                    for t in range(SP2):
                        mm = pe.transpose(y_whole[:, t, c * P:(c + 1) * P], yT[:, r, c, t * P:(t + 1) * P], ident[:, :])
                mm.then_inc(yr_done, 1)

            def product(dst, w, x, start, stop):
                mm = pe.matmul(dst, w[0], x[0], start=start, stop=False)
                mm = pe.matmul(dst, w[0], x[1], start=False, stop=False)
                return pe.matmul(dst, w[1], x[0], start=False, stop=stop)

            def expert(e, r):
                pe.wait_ge(w1_lo, (e + 1) * WQ)
                pe.wait_ge(x_lo, e + 1)
                for j in range(HC):
                    if not (first(e) and j < 3):
                        pe.wait_ge(h_done, e * HC + max(j - 2, 0))
                    for c in range(DC):
                        w = [p[:, c * HID + j * P:c * HID + (j + 1) * P] for p in w1p[r]]
                        x = [p[:, c * NS:(c + 1) * NS] for p in xp[r]]
                        mm = product(bank[j % 3][:, 0:NS], w, x, c == 0, c == DC - 1)
                    mm.then_inc(l1_done, 1)
                if not first(e):
                    slot_rows(e - 1, 1 - r)
                if not last(e):
                    slots_across(e + 1, 1 - r)
                pe.wait_ge(w2_lo_pool, (e + 1) * (WQ // 2))
                pe.wait_ge(w2_lo_dve, (e + 1) * (WQ // 2))
                for c in range(DC):
                    for j in range(HC):
                        if c == 0:
                            pe.wait_ge(h_lo, e * HC + j + 1)
                        w = [p[:, j * D + c * P:j * D + (c + 1) * P] for p in w2p[r]]
                        mm = product(bank[4 + c][:, 0:NS], w, [p[:, :] for p in hp[j]], j == 0, j == HC - 1)
                    mm.then_inc(l2_done, 1)

            slots_across(0, 0)
            pe.wait_ge(padded, 1)
            expert_loop(pe, expert)
            slot_rows(E - 1, 1)


def kernel(x, L0_tok_W, L0_tok_b, L0_attn_Wq, L0_attn_Wk, L0_attn_Wv, L0_attn_Wo, L0_attn_lambda_q1,
           L0_attn_lambda_k1, L0_attn_lambda_q2, L0_attn_lambda_k2, L0_attn_gamma, L0_attn_beta,
           L0_ffn_Wg, L0_ffn_W1, L0_ffn_b1, L0_ffn_W2, L0_ffn_b2):
    import concourse.bacc as _bacc
    from concourse.bass_utils import run_bass_kernel_spmd as _run

    def rows_first(w):
        return np.ascontiguousarray(w.reshape(w.shape[0] // P, P, w.shape[1]).transpose(1, 0, 2))

    a = SIDE // PATCH
    img = np.asarray(x).reshape(IMGS, CH, a, PATCH, a, PATCH).transpose(3, 5, 1, 0, 2, 4).reshape(IN, N)
    xh = np.ascontiguousarray(img.reshape(IC, P, G, P).transpose(1, 2, 0, 3))
    n = np.asarray
    ins = {
        "xh": xh,
        "wt": rows_first(n(L0_tok_W).T),
        "tok_b": n(L0_tok_b),
        "wq": rows_first(n(L0_attn_Wq)), "wk": rows_first(n(L0_attn_Wk)),
        "wv": rows_first(n(L0_attn_Wv)), "wo": rows_first(n(L0_attn_Wo)),
        "lam": np.stack([n(L0_attn_lambda_q1), n(L0_attn_lambda_k1), n(L0_attn_lambda_q2),
                         n(L0_attn_lambda_k2)]).reshape(2, 2, HD),
        "gamma": n(L0_attn_gamma), "beta": n(L0_attn_beta),
        "wg": rows_first(n(L0_ffn_Wg)),
        "w1": np.ascontiguousarray(n(L0_ffn_W1).reshape(E, DC, P, HID).transpose(0, 2, 1, 3)).reshape(E, P, DC * HID),
        "b1": np.ascontiguousarray(n(L0_ffn_b1).reshape(E, HC, P).transpose(2, 0, 1)),
        "w2": np.ascontiguousarray(n(L0_ffn_W2).reshape(E, HC, P, D).transpose(0, 2, 1, 3)).reshape(E, P, HC * D),
        "b2": np.ascontiguousarray(n(L0_ffn_b2).reshape(E, DC, P).transpose(2, 0, 1)),
    }
    nc = _bacc.Bacc("TRN2", target_bir_lowering=False, num_devices=1)
    args = [nc.dram_tensor(f"in_{k}", v.shape, F32, kind="ExternalInput").ap() for k, v in ins.items()]
    out = nc.dram_tensor("out", (N + CAP, D), F32, kind="ExternalOutput").ap()
    vit_tower(nc, *args, out)
    r = _run(nc, [{f"in_{k}": v for k, v in ins.items()}], core_ids=[0])
    return r.results[0]["out"][:N].reshape(IMGS, S, D)
```
